# Optimizing a Trainium2 kernel written in Bass

```python
import numpy as np
import jax
import jax.numpy as jnp

def _softmax(x, axis=-1):
    return jax.nn.softmax(x, axis=axis)

def _gelu(x):
    return jax.nn.gelu(x, approximate=True)

def _silu(x):
    return jax.nn.silu(x)

def _sigmoid(x):
    return jax.nn.sigmoid(x)

def _layernorm(x, axis=-1, eps=1e-05):
    m = jnp.mean(x, axis=axis, keepdims=True)
    v = jnp.var(x, axis=axis, keepdims=True)
    return (x - m) / jnp.sqrt(v + eps)

def _scatter_add(tgt, idx, src, axis=0):
    return tgt.at[idx].add(src)

def _segment_sum(src, seg, n):
    return jax.ops.segment_sum(src, seg, n)
kernel_name = 'mk_flamingo_gated_d1_seqx_r8_c86733'

def setup_inputs(seed: int=0):
    np.random.seed(seed)
    _w = jnp.asarray

    def _rec_inputs():
        import jax
        import jax.numpy as jnp
        _rk = jax.random.key(seed)
        x = -0.0003929 + 0.9999 * jax.random.normal(jax.random.fold_in(_rk, 1), (32, 56, 128), jnp.float32)
        _lenS = 56 - jax.random.randint(jax.random.fold_in(_rk, 7), (32,), 0, max(1, 56 // 4) + 1, jnp.int32)
        _lenS2 = 1500 - jax.random.randint(jax.random.fold_in(_rk, 8), (32,), 0, max(1, 1500 // 4) + 1, jnp.int32)
        _ctx_768P = jax.random.normal(jax.random.fold_in(_rk, 11), (32, 16, 96), jnp.float32)
        _ctx_768c = jax.random.dirichlet(jax.random.fold_in(_rk, 511), 0.3 * jnp.ones((16,), jnp.float32), (32, 1500))
        _ctx_768t = jnp.einsum('bsk,bkd->bsd', _ctx_768c, _ctx_768P)
        _ctx_768t = _ctx_768t * jax.lax.rsqrt(jnp.mean(jnp.square(_ctx_768t)) + 1e-12) * 0.953939
        ctx_768 = 2.09791e-05 + 1.00001 * (_ctx_768t + 0.3 * jax.random.normal(jax.random.fold_in(_rk, 611), (32, 1500, 96), jnp.float32))
        _g = jax.random.normal(jax.random.fold_in(_rk, 9001), (2, 1), jnp.float32)
        _g = jnp.sign(_g) * jnp.maximum(jnp.abs(_g), 1.0) + (_g == 0) * 1.0
        g_xattn = _g[0]
        g_ffn = _g[1]
        return (x, ctx_768, g_xattn, g_ffn)
    x, ctx_768, g_xattn, g_ffn = _rec_inputs()

    def _L0_xattn_setup():
        import jax, jax.numpy as jnp
        import numpy as np
        QUERY_DIM = 128
        KEY_DIM = 96
        NUM_HEADS = 16
        HEAD_DIM = QUERY_DIM // NUM_HEADS
        SCALE = HEAD_DIM ** (-0.5)
        key = jax.random.key(seed)
        ks = jax.random.split(key, 11)
        B, Nq, Nk = (4, 512, 128)
        s_q = QUERY_DIM ** (-0.5)
        s_k = KEY_DIM ** (-0.5)
        return {'query': jax.random.normal(ks[0], (B, Nq, QUERY_DIM), jnp.float32), 'key': jax.random.normal(ks[1], (B, Nk, KEY_DIM), jnp.float32), 'value': jax.random.normal(ks[2], (B, Nk, KEY_DIM), jnp.float32), 'Wq': jax.random.normal(ks[3], (QUERY_DIM, QUERY_DIM), jnp.float32) * s_q, 'bq': jnp.zeros((QUERY_DIM,), jnp.float32), 'Wk': jax.random.normal(ks[4], (KEY_DIM, QUERY_DIM), jnp.float32) * s_k, 'bk': jnp.zeros((QUERY_DIM,), jnp.float32), 'Wv': jax.random.normal(ks[5], (KEY_DIM, QUERY_DIM), jnp.float32) * s_k, 'bv': jnp.zeros((QUERY_DIM,), jnp.float32), 'Wo': jax.random.normal(ks[6], (QUERY_DIM, QUERY_DIM), jnp.float32) * s_q, 'bo': jnp.zeros((QUERY_DIM,), jnp.float32)}
    _L0_xattn_all = _L0_xattn_setup()
    _L0_xattn_in = {k: v for k, v in _L0_xattn_all.items() if k in ('Wq', 'bq', 'Wk', 'bk', 'Wv', 'bv', 'Wo', 'bo')}
    del _L0_xattn_all

    def _L0_ffn_setup():
        import jax, jax.numpy as jnp
        import numpy as np
        B, T, D, H, E, K = (2, 256, 128, 512, 8, 2)
        EPS = 1e-12

        def moe_forward(x, Wg, bg, W1, b1, W2, b2):
            gates = jax.nn.softmax(x @ Wg + bg, axis=-1)
            _, top_idx = jax.lax.top_k(gates, K)
            mask = jax.nn.one_hot(top_idx, E, dtype=gates.dtype).sum(axis=-2)
            g = gates * mask
            g = g / jnp.maximum(jnp.sum(jnp.abs(g), axis=-1, keepdims=True), EPS)
            h = jnp.einsum('btd,edh->bteh', x, W1) + b1[None, None]
            h = jax.nn.gelu(h, approximate=False)
            eo = jnp.einsum('bteh,ehd->bted', h, W2) + b2[None, None]
            return jnp.einsum('bte,bted->btd', g, eo)
        key = jax.random.key(seed)
        ks = jax.random.split(key, 8)
        s_d = 1.0 / np.sqrt(D)
        s_h = 1.0 / np.sqrt(H)
        return {'x': jax.random.normal(ks[0], (B, T, D), dtype=jnp.float32), 'Wg': jax.random.uniform(ks[1], (D, E), jnp.float32, -s_d, s_d), 'bg': jax.random.uniform(ks[2], (E,), jnp.float32, -s_d, s_d), 'W1': jax.random.uniform(ks[3], (E, D, H), jnp.float32, -s_d, s_d), 'b1': jax.random.uniform(ks[4], (E, H), jnp.float32, -s_d, s_d), 'W2': jax.random.uniform(ks[5], (E, H, D), jnp.float32, -s_h, s_h), 'b2': jax.random.uniform(ks[6], (E, D), jnp.float32, -s_h, s_h)}
    _L0_ffn_all = _L0_ffn_setup()
    _L0_ffn_in = {k: v for k, v in _L0_ffn_all.items() if k in ('Wg', 'bg', 'W1', 'b1', 'W2', 'b2')}
    del _L0_ffn_all
    return {'x': x, 'ctx_768': ctx_768, 'g_xattn': g_xattn, 'g_ffn': g_ffn, 'L0_xattn_Wq': _L0_xattn_in['Wq'], 'L0_xattn_bq': _L0_xattn_in['bq'], 'L0_xattn_Wk': _L0_xattn_in['Wk'], 'L0_xattn_bk': _L0_xattn_in['bk'], 'L0_xattn_Wv': _L0_xattn_in['Wv'], 'L0_xattn_bv': _L0_xattn_in['bv'], 'L0_xattn_Wo': _L0_xattn_in['Wo'], 'L0_xattn_bo': _L0_xattn_in['bo'], 'L0_ffn_Wg': _L0_ffn_in['Wg'], 'L0_ffn_bg': _L0_ffn_in['bg'], 'L0_ffn_W1': _L0_ffn_in['W1'], 'L0_ffn_b1': _L0_ffn_in['b1'], 'L0_ffn_W2': _L0_ffn_in['W2'], 'L0_ffn_b2': _L0_ffn_in['b2']}

def reference(x, ctx_768, g_xattn, g_ffn, L0_xattn_Wq, L0_xattn_bq, L0_xattn_Wk, L0_xattn_bk, L0_xattn_Wv, L0_xattn_bv, L0_xattn_Wo, L0_xattn_bo, L0_ffn_Wg, L0_ffn_bg, L0_ffn_W1, L0_ffn_b1, L0_ffn_W2, L0_ffn_b2):
    import jax
    import jax.numpy as jnp

    def _L0_xattn_ref(query, key, value, Wq, bq, Wk, bk, Wv, bv, Wo, bo):
        import jax, jax.numpy as jnp
        import numpy as np
        QUERY_DIM = 128
        KEY_DIM = 96
        NUM_HEADS = 16
        HEAD_DIM = QUERY_DIM // NUM_HEADS
        SCALE = HEAD_DIM ** (-0.5)
        B, Nq, _ = query.shape
        Nk = key.shape[1]
        q = (query @ Wq + bq).reshape(B, Nq, NUM_HEADS, HEAD_DIM).transpose(0, 2, 1, 3)
        k = (key @ Wk + bk).reshape(B, Nk, NUM_HEADS, HEAD_DIM).transpose(0, 2, 1, 3)
        v = (value @ Wv + bv).reshape(B, Nk, NUM_HEADS, HEAD_DIM).transpose(0, 2, 1, 3)
        attn = jnp.einsum('bhqd,bhkd->bhqk', q, k) * SCALE
        attn = jax.nn.softmax(attn, axis=-1)
        out = jnp.einsum('bhqk,bhkd->bhqd', attn, v)
        out = out.transpose(0, 2, 1, 3).reshape(B, Nq, QUERY_DIM)
        return out @ Wo + bo

    def _L0_ffn_ref(x, Wg, bg, W1, b1, W2, b2):
        import jax, jax.numpy as jnp
        import numpy as np
        B, T, D, H, E, K = (2, 256, 128, 512, 8, 2)
        EPS = 1e-12

        def moe_forward(x, Wg, bg, W1, b1, W2, b2):
            gates = jax.nn.softmax(x @ Wg + bg, axis=-1)
            _, top_idx = jax.lax.top_k(gates, K)
            mask = jax.nn.one_hot(top_idx, E, dtype=gates.dtype).sum(axis=-2)
            g = gates * mask
            g = g / jnp.maximum(jnp.sum(jnp.abs(g), axis=-1, keepdims=True), EPS)
            h = jnp.einsum('btd,edh->bteh', x, W1) + b1[None, None]
            h = jax.nn.gelu(h, approximate=False)
            eo = jnp.einsum('bteh,ehd->bted', h, W2) + b2[None, None]
            return jnp.einsum('bte,bted->btd', g, eo)
        return moe_forward(x, Wg, bg, W1, b1, W2, b2)
    x = x + jnp.tanh(g_xattn[0]) * _L0_xattn_ref(_layernorm(x, axis=-1), ctx_768, ctx_768, L0_xattn_Wq, L0_xattn_bq, L0_xattn_Wk, L0_xattn_bk, L0_xattn_Wv, L0_xattn_bv, L0_xattn_Wo, L0_xattn_bo)
    x = x + jnp.tanh(g_ffn[0]) * _L0_ffn_ref(_layernorm(x, axis=-1), L0_ffn_Wg, L0_ffn_bg, L0_ffn_W1, L0_ffn_b1, L0_ffn_W2, L0_ffn_b2)
    return x

_drawn_inputs = setup_inputs


def setup_inputs(seed=0):
    import zlib

    import numpy as np

    out = dict(_drawn_inputs(seed))
    spreads = {'L0_xattn_bq': (0.0, 0.319),
     'L0_xattn_bk': (0.0, 0.8),
     'L0_xattn_bv': (0.0, 0.1),
     'L0_xattn_bo': (0.0, 0.1)}
    factors = {'L0_ffn_b1': 4.862, 'L0_ffn_b2': 3.496}
    for name, (base, spread) in spreads.items():
        noise = np.random.default_rng([zlib.crc32(name.encode()), seed]).standard_normal(out[name].shape)
        drawn = base * np.exp(spread * noise) if base else spread * noise
        out[name] = jnp.asarray(drawn.astype(out[name].dtype))
    for name, factor in factors.items():
        out[name] = (out[name] * factor).astype(out[name].dtype)
    return out
```

```python
from contextlib import ExitStack

import concourse.bass as bass
from concourse import mybir

F32 = mybir.dt.float32
F32R = mybir.dt.float32r
ALU = mybir.AluOpType
ACT = mybir.ActivationFunctionType
AX_X = mybir.AxisListType.X

P = 128


def gated_xattn_moe(nc, x, ctx, g_xattn, g_ffn, Wq, bq, Wk, bk, Wv, bv, Wo, bo,
                    Wg, bg, W1, b1, W2, b2, out):
    B, NQ, D = x.shape
    _, NK, KD = ctx.shape
    HEADS = 16
    HD = D // HEADS
    SCALE = float(HD) ** -0.5
    LN_EPS, GATE_EPS = 1e-5, 1e-12
    KT = 12
    KP = NK // KT
    HQ = HEADS * NQ
    HALF = HQ // 2
    CR = KD + 2
    GT = 4
    NG = KT // GT
    MT = HQ // P
    MC = 3
    CK = NK // MC
    PAIRS = HEADS // 2
    PQ = 2 * NQ
    VW = 32
    J, R = 4, 2
    TOK = B * NQ
    TT = TOK // P
    NE, HID = W1.shape[0], W1.shape[2]
    SL = HID // P
    CH = TOK // HALF
    TOP = 2
    GATE_STEPS = 19
    SMALL = 15
    assert KT * KP == NK and MT * P == HQ and TT * P == TOK and CH * HALF == TOK
    assert MC * CK == NK and D == P and NQ % TT == 0

    with ExitStack() as stack:
        def sb(name, shape, dt=F32):
            return stack.enter_context(nc.sbuf_tensor(name, shape, dt))

        def psum(name, shape):
            return stack.enter_context(nc.psum_tensor(name, shape, F32))

        def sem(name):
            return stack.enter_context(nc.semaphore(name))

        x1_dram = nc.dram_tensor("x1_scratch", [TOK, D], F32, kind="Internal").ap()

        scores_ps = psum("scores_ps", [P, 2, 2, 512])
        prep_ps = psum("prep_ps", [P, 2, 512])
        pv_ps = psum("pv_ps", [P, 512])
        misc_ps = psum("misc_ps", [P, 512])

        ident = sb("ident", [P, P])
        head_mask = sb("head_mask", [P, HEADS])
        wq = sb("wq", [P, D])
        bq_c = sb("bq_c", [P, 1])
        wk_rows = sb("wk_rows", [CR, D])
        wk_fold = sb("wk_fold", [P, CR])
        wv_rows = sb("wv_rows", [CR, D])
        wv_h = sb("wv_h", [CR, D], F32R)
        wv_l = sb("wv_l", [CR, D], F32R)
        wo = sb("wo", [P, D])
        gate_in = sb("gate_in", [P, 2])
        gate_tanh = sb("gate_tanh", [P, 2])
        bo_b = sb("bo_b", [NQ, D])
        bo_gated = sb("bo_gated", [NQ, D])
        wg = sb("wg", [P, NE])
        wg_h = sb("wg_h", [P, NE], F32R)
        wg_l = sb("wg_l", [P, NE], F32R)
        bg_b = sb("bg_b", [P, NE])
        w1 = [sb(f"w1_{k}", [P, HID]) for k in range(2)]
        w1_h = sb("w1_h", [P, NE, HID], F32R)
        w1_l = sb("w1_l", [P, NE, HID], F32R)
        b1_rows = sb("b1_rows", [NE * SL, P])
        b1_c = sb("b1_c", [P, NE * SL])
        w2 = sb("w2", [P, NE * SL, D])
        b2_r = sb("b2_r", [2 * NE, D])
        b2_h = sb("b2_h", [2 * NE, D], F32R)
        b2_l = sb("b2_l", [2 * NE, D], F32R)
        lower = sb("lower", [P, NE, NE])
        expert_pick = sb("expert_pick", [2 * NE, NE, P], F32R)
        pick_f = sb("pick_f", [2 * NE, NE, P])

        tok = sb("tok", [P, TT, D])
        tok_c = sb("tok_c", [P, TT, D])
        y_sb = tok_c
        gated = tok_c[:].rearrange("p t d -> p (t d)")[:, 0:3 * HALF].rearrange("p (n c) -> p n c", n=3)
        ln_sum = sb("ln_sum", [P, TT])
        ln_mean = sb("ln_mean", [P, TT])
        ln_sq = sb("ln_sq", [P, TT])
        ln_var = sb("ln_var", [P, TT])
        ln_std = sb("ln_std", [P, TT])
        ln_rstd = sb("ln_rstd", [P, TT])
        xnT = sb("xnT", [P, TOK])
        squares = xnT[:].rearrange("p (t d) -> p t d", t=TT)
        qT_all = sb("qT_all", [P, TOK])
        cmp_gt = qT_all[:, 0:HALF * 2].rearrange("p (t n) -> p t n", t=TT)
        cmp_eq = qT_all[:, HALF * 2:].rearrange("p (t n) -> p t n", t=TT)
        gelu = qT_all[:, 0:3 * HALF].rearrange("p (n c) -> p n c", n=3)
        x2_h = sb("x2_h", [P, TOK], F32R)
        x2_l = sb("x2_l", [P, TOK], F32R)

        nat = [sb(f"nat{k}", [KP, KT, CR]) for k in range(2)]
        ctx_h = [sb(f"ctx_h{k}", [CR, KT, KP], F32R) for k in range(2)]
        ctx_l = [sb(f"ctx_l{k}", [CR, KT, KP], F32R) for k in range(2)]
        q_h = [sb(f"q_h{k}", [CR, HQ], F32R) for k in range(2)]
        q_l = [sb(f"q_l{k}", [CR, HQ], F32R) for k in range(2)]
        val = [sb(f"val{k}", [KP, KT, PAIRS, VW]) for k in range(2)]
        prob = [sb(f"prob{k}", [KP, HQ]) for k in range(2)]
        x_res = [sb(f"x_res{k}", [NQ, D]) for k in range(2)]
        x_bo = [sb(f"x_bo{k}", [NQ, D]) for k in range(2)]
        x1 = [sb(f"x1_{k}", [NQ, D]) for k in range(2)]
        q_diag = sb("q_diag", [P, HEADS, NQ])
        part_max = sb("part_max", [P, MT, MC])
        neg_max = sb("neg_max", [P, MT])
        acc = sb("acc", [P, R, 2, NQ])
        den_inv = sb("den_inv", [NQ, HEADS])
        heads = sb("heads", [NQ, D])
        headsT = sb("headsT", [P, NQ])

        logit = sb("logit", [P, TT, NE])
        lmax = sb("lmax", [P, TT])
        lexp = sb("lexp", [P, TT, NE])
        lsum = sb("lsum", [P, TT])
        gates = sb("gates", [P, TT, NE])
        rank = sb("rank", [P, TT, NE])
        gate_hl = sb("gate_hl", [P, TT, 2 * NE], F32R)
        gT2 = sb("gT2", [2 * NE, TOK], F32R)

        small_loaded = sem("small_loaded")
        tok_loaded = sem("tok_loaded")
        w1_loaded = [sem(f"w1_loaded{k}") for k in range(2)]
        w2_loaded = sem("w2_loaded")
        nat_loaded = [sem(f"nat_loaded{k}") for k in range(2)]
        x_res_loaded = [sem(f"x_res_loaded{k}") for k in range(2)]
        x1_stored = [sem(f"x1_stored{k}") for k in range(2)]
        x1_loaded = sem("x1_loaded")
        out_stored = sem("out_stored")
        consts_ready = sem("consts_ready")
        frames_ready = sem("frames_ready")
        ln_step = sem("ln_step")
        ln_act = sem("ln_act")
        xn_transposed = sem("xn_transposed")
        xn_copied = sem("xn_copied")
        q_projected = sem("q_projected")
        q_copied = sem("q_copied")
        wk_transposed = sem("wk_transposed")
        wk_copied = sem("wk_copied")
        weights_split = sem("weights_split")
        tanh_ready = sem("tanh_ready")
        bo_ready = sem("bo_ready")
        ctx_transposed = sem("ctx_transposed")
        ctx_h_ready = sem("ctx_h_ready")
        ctx_l_ready = sem("ctx_l_ready")
        q_diag_ready = sem("q_diag_ready")
        q_folded = sem("q_folded")
        q_h_ready = sem("q_h_ready")
        q_l_ready = sem("q_l_ready")
        max_scored = sem("max_scored")
        max_reduced = sem("max_reduced")
        neg_max_ready = sem("neg_max_ready")
        max_row_done = sem("max_row_done")
        max_row_copied = sem("max_row_copied")
        val_done = sem("val_done")
        val_copied = sem("val_copied")
        scored = sem("scored")
        exp_done = sem("exp_done")
        pv_done = sem("pv_done")
        acc_copied = sem("acc_copied")
        acc_transposed = sem("acc_transposed")
        den_ready = sem("den_ready")
        heads_ready = sem("heads_ready")
        heads_transposed = sem("heads_transposed")
        headsT_copied = sem("headsT_copied")
        projected = sem("projected")
        x_bo_ready = sem("x_bo_ready")
        x1_ready = sem("x1_ready")
        w1_h_ready = sem("w1_h_ready")
        w1_split = sem("w1_split")
        x2_h_ready = sem("x2_h_ready")
        x2_l_ready = sem("x2_l_ready")
        logits_done = sem("logits_done")
        gate_step = sem("gate_step")
        gates_transposed = sem("gates_transposed")
        gates_copied = sem("gates_copied")
        hidden_done = sem("hidden_done")
        gelu_done = sem("gelu_done")
        spread_done = sem("spread_done")
        gated_done = sem("gated_done")
        summed = sem("summed")
        sum_copied = sem("sum_copied")
        y_transposed = sem("y_transposed")
        y_ready = sem("y_ready")

        ctx_v = ctx.rearrange("b (p t) c -> b p t c", t=KT)
        x_tok = x.rearrange("b q d -> (b q) d").rearrange("(p t) d -> p t d", t=TT)
        x1_b = x1_dram.rearrange("(b q) d -> b q d", q=NQ)
        x1_tok = x1_dram.rearrange("(p t) d -> p t d", t=TT)
        out_tok = out.rearrange("b q d -> (b q) d").rearrange("(p t) d -> p t d", t=TT)

        def row(v):
            return v.rearrange("(a n) -> a n", a=1)

        def spread(v, shape):
            return v.to_broadcast(shape)

        def batches(engine, main):
            main(0, 0, True, False)
            with engine.Fori(0, (B - 2) // 2) as i:
                main(2 * i + 1, 1, False, False)
                main(2 * i + 2, 0, False, False)
            main(B - 1, 1, False, True)

        block = stack.enter_context(nc.Block())

        @block.sync
        def _(sp):
            sp.dma_start(tok[:], x_tok).then_inc(tok_loaded, 16)
            for b in range(2):
                sp.dma_start(nat[b][:, :, 1:1 + KD], ctx_v[b]).then_inc(nat_loaded[b], 16)
                sp.dma_start(x_res[b][:], x[b]).then_inc(x_res_loaded[b], 16)

            def load_ctx(b, k):
                sp.wait_ge(ctx_transposed, NG * b - NG)
                sp.dma_start(nat[k][:, :, 1:1 + KD], ctx_v[b]).then_inc(nat_loaded[k], 16)

            def load_x(b, k):
                sp.wait_ge(x_bo_ready, b - 1)
                sp.dma_start(x_res[k][:], x[b]).then_inc(x_res_loaded[k], 16)

            def store(b, k):
                sp.wait_ge(x1_ready, b + 1)
                sp.dma_start(x1_b[b], x1[k][:]).then_inc(x1_stored[k], 16)

            for b in (2, 3):
                load_ctx(b, b % 2)
                load_x(b, b % 2)
            with sp.Fori(0, (B - 4) // 2) as i:
                for k in range(2):
                    load_ctx(2 * i + 4 + k, k)
                    store(2 * i + k, k)
                    load_x(2 * i + 4 + k, k)
            store(B - 4, 0)
            store(B - 3, 1)
            for e in range(NE):
                if e >= 2:
                    sp.wait_ge(w1_split, e - 1)
                sp.dma_start(w1[e % 2][:], W1[e]).then_inc(w1_loaded[e % 2], 16)
            sp.dma_start(w2[:], W2.rearrange("e (s p) d -> p (e s) d", p=P)).then_inc(w2_loaded, 16)
            for b in range(B - 2, B):
                store(b, b % 2)
            for k in range(2):
                sp.wait_ge(x1_stored[k], 16 * (B // 2))
            sp.dma_start(tok[:], x1_tok).then_inc(x1_loaded, 16)
            for n in range(4):
                sp.wait_ge(y_ready, n + 1)
                tiles = slice(4 * n, min(4 * n + 4, TT))
                sp.dma_start(out_tok[:, tiles], y_sb[:, tiles]).then_inc(out_stored, 16)
            sp.wait_ge(out_stored, 64)

        @block.gpsimd
        def _(pool):
            for k in range(2):
                for c in (0, CR - 1):
                    last = nc.gpsimd.memset(nat[k][:, :, c:c + 1], 1.0)
                last.then_inc(frames_ready, 1)
            nc.gpsimd.memset(ident[:], 0.0)
            nc.gpsimd.memset(head_mask[:], 1.0)
            nc.gpsimd.memset(lower[:], 1.0)
            nc.gpsimd.memset(pick_f[:], 0.0).then_inc(frames_ready, 1)
            pool.wait_ge(frames_ready, 3)
            nc.gpsimd.affine_select(out=ident[:], in_=ident[:], compare_op=ALU.not_equal, fill=1.0,
                                    base=0, pattern=[[-1, P]], channel_multiplier=1).then_inc(consts_ready, 1)
            nc.gpsimd.affine_select(out=head_mask[:], in_=head_mask[:], compare_op=ALU.is_ge, fill=0.0,
                                    base=0, pattern=[[-HD, HEADS]], channel_multiplier=1).then_inc(consts_ready, 1)
            pool.wait_ge(consts_ready, 2)
            nc.gpsimd.affine_select(out=head_mask[:], in_=head_mask[:], compare_op=ALU.is_ge, fill=0.0,
                                    base=HD - 1, pattern=[[HD, HEADS]], channel_multiplier=-1).then_inc(consts_ready, 1)
            nc.gpsimd.affine_select(out=lower[:], in_=lower[:], compare_op=ALU.is_gt, fill=0.0,
                                    base=0, pattern=[[1, NE], [-1, NE]], channel_multiplier=0).then_inc(consts_ready, 1)
            nc.gpsimd.affine_select(out=pick_f[:], in_=pick_f[:], compare_op=ALU.not_equal, fill=1.0,
                                    base=0, pattern=[[-1, NE], [0, P]], channel_multiplier=1).then_inc(consts_ready, 1)
            pool.wait_ge(consts_ready, 5)
            nc.gpsimd.affine_select(out=pick_f[:], in_=pick_f[:], compare_op=ALU.not_equal, fill=1.0,
                                    base=-NE, pattern=[[-1, NE], [0, P]], channel_multiplier=1).then_inc(consts_ready, 1)
            pool.wait_ge(consts_ready, 6)
            nc.gpsimd.memset(val[0][:, :, :, HD * 2:VW], 1.0)
            nc.gpsimd.memset(val[1][:, :, :, HD * 2:VW], 1.0).then_inc(frames_ready, 1)

            pool.wait_ge(q_copied, CH)
            pool.wait_ge(bo_ready, 1)

            def diagonal(b, k, first):
                if not first:
                    pool.wait_ge(q_folded, 2 * b)
                nc.gpsimd.tensor_tensor(
                    out=q_diag[:],
                    in0=qT_all[:, bass.ds(b * NQ, NQ)].rearrange("p (a q) -> p a q", a=1).to_broadcast([P, HEADS, NQ]),
                    in1=head_mask[:].rearrange("p (h a) -> p h a", a=1).to_broadcast([P, HEADS, NQ]),
                    op=ALU.mult).then_inc(q_diag_ready, 1)
                pool.wait_ge(x_res_loaded[k], 16 * (b // 2) + 16 if isinstance(b, int) else 8 * (b - k) + 16)
                if not (first or isinstance(b, int) and b < 2):
                    pool.wait_ge(x1_ready, b - 1)
                    pool.wait_ge(x1_stored[k], 8 * (b - k))
                nc.gpsimd.tensor_tensor(out=x_bo[k][:], in0=x_res[k][:], in1=bo_gated[:],
                                        op=ALU.add).then_inc(x_bo_ready, 1)

            diagonal(0, 0, True)
            diagonal(1, 1, False)
            with pool.Fori(0, (B - 2) // 2) as i:
                for k in range(2):
                    diagonal(2 * i + 2 + k, k, False)

            for e in range(NE):
                pool.wait_ge(w1_loaded[e % 2], 16 * (e // 2) + 16)
                nc.gpsimd.tensor_copy(w1_h[:, e], w1[e % 2][:]).then_inc(w1_h_ready, 1)
                pool.wait_ge(w1_h_ready, e + 1)
                nc.gpsimd.tensor_tensor(out=w1_l[:, e], in0=w1[e % 2][:], in1=w1_h[:, e].bitcast(F32),
                                        op=ALU.subtract).then_inc(w1_split, 1)

        @block.scalar
        def _(act):
            act.dma_start(gate_in[:, 0:1], row(g_xattn).to_broadcast([P, 1])).then_inc(small_loaded, 16)
            act.dma_start(gate_in[:, 1:2], row(g_ffn).to_broadcast([P, 1])).then_inc(small_loaded, 16)
            act.dma_start(wq[:], Wq).then_inc(small_loaded, 16)
            act.dma_start(bq_c[:], bq.rearrange("(p a) -> p a", a=1)).then_inc(small_loaded, 16)
            act.dma_start(wk_rows[1:1 + KD, :], Wk).then_inc(small_loaded, 16)
            act.dma_start(wk_rows[CR - 1:CR, :], row(bk)).then_inc(small_loaded, 16)
            act.dma_start(wv_rows[1:1 + KD, :], Wv).then_inc(small_loaded, 16)
            act.dma_start(wv_rows[CR - 1:CR, :], row(bv)).then_inc(small_loaded, 16)
            act.dma_start(bo_b[:], row(bo).to_broadcast([NQ, D])).then_inc(small_loaded, 16)
            act.dma_start(wo[:], Wo).then_inc(small_loaded, 16)
            act.dma_start(wg[:], Wg).then_inc(small_loaded, 16)
            act.dma_start(bg_b[:], row(bg).to_broadcast([P, NE])).then_inc(small_loaded, 16)
            act.dma_start(b1_rows[:], b1.rearrange("e (s p) -> (e s) p", p=P)).then_inc(small_loaded, 16)
            act.dma_start(b2_r[0:NE, :], b2).then_inc(small_loaded, 16)
            act.dma_start(b2_r[NE:2 * NE, :], b2).then_inc(small_loaded, 16)
            act.wait_ge(small_loaded, SMALL * 16)

            def norm_act(n):
                act.wait_ge(ln_step, 8 * n + 3)
                nc.scalar.activation(squares, tok_c[:], ACT.Square).then_inc(ln_act, 1)
                act.wait_ge(ln_step, 8 * n + 5)
                nc.scalar.activation(ln_std[:], ln_var[:], ACT.Sqrt).then_inc(ln_act, 1)

            norm_act(0)
            nc.scalar.activation(gate_tanh[:], gate_in[:], ACT.Tanh).then_inc(tanh_ready, 1)
            act.wait_ge(wk_transposed, 1)
            nc.scalar.activation(b1_c[:], misc_ps[:, P:P + NE * SL], ACT.Copy)
            nc.scalar.activation(wk_fold[:], misc_ps[:, 0:CR], ACT.Copy).then_inc(wk_copied, 1)
            xnT_tok = xnT[:].rearrange("f (p t) -> f t p", t=TT)
            for n in range(4):
                act.wait_ge(xn_transposed, n + 1)
                w = min(4, TT - 4 * n)
                nc.scalar.activation(xnT_tok[:, 4 * n:4 * n + w, :],
                                     scores_ps[:, n // 2, n % 2, 0:w * P].rearrange("f (t p) -> f t p", p=P),
                                     ACT.Copy).then_inc(xn_copied, 1)
            for n in range(CH):
                act.wait_ge(q_projected, n + 1)
                nc.scalar.activation(qT_all[:, n * HALF:(n + 1) * HALF], scores_ps[:, n // 2, n % 2, 0:HALF],
                                     ACT.Identity, bias=bq_c[:]).then_inc(q_copied, 1)

            def ctx_high(b, k, g):
                act.wait_ge(ctx_transposed, NG * b + g + 1)
                nc.scalar.activation(ctx_h[k][:, GT * g:GT * g + GT, :],
                                     prep_ps[0:CR, g % 2, 0:GT * KP].rearrange("c (t p) -> c t p", p=KP),
                                     ACT.Copy).then_inc(ctx_h_ready, 1)

            def q_high(b, k, n):
                act.wait_ge(q_folded, 2 * b + n + 1)
                nc.scalar.activation(q_h[k][:, n * HALF:(n + 1) * HALF], prep_ps[0:CR, 1 - n, 0:HALF],
                                     ACT.Copy).then_inc(q_h_ready, 1)

            def finish_acc(b):
                act.wait_ge(pv_done, KT * b + KT)
                nc.scalar.activation(acc[:].rearrange("p r a q -> p (r a q)"), pv_ps[:, 0:R * PQ],
                                     ACT.Copy).then_inc(acc_copied, 1)

            def finish_heads(b):
                act.wait_ge(heads_transposed, b + 1)
                nc.scalar.activation(headsT[:], misc_ps[:, 0:NQ], ACT.Copy).then_inc(headsT_copied, 1)

            for g in range(NG):
                ctx_high(0, 0, g)
            for n in range(2):
                q_high(0, 0, n)

            def main(b, k, first, last):
                for t in range(KT):
                    act.wait_ge(scored, KT * b + t + 1)
                    if not (first and t < 2):
                        act.wait_ge(pv_done, KT * b + t - 1)
                    nc.scalar.activation(prob[t % 2][:].rearrange("p (n q) -> p n q", n=2),
                                         scores_ps[0:KP, t % 2, :, 0:HALF], ACT.Exp,
                                         scale=SCALE).then_inc(exp_done, 1)
                    if t == 0 and not first:
                        finish_acc(b - 1)
                    if t == 0 and not last:
                        ctx_high(b + 1, 1 - k, 0)
                        ctx_high(b + 1, 1 - k, 1)
                    if t == 1 and not last:
                        ctx_high(b + 1, 1 - k, 2)
                    if t in (2, 3) and not last:
                        q_high(b + 1, 1 - k, t - 2)
                    if t == 3 and not first:
                        finish_heads(b - 1)

            batches(act, main)
            finish_acc(B - 1)
            finish_heads(B - 1)

            norm_act(1)
            for n in range(4):
                act.wait_ge(xn_transposed, 4 + n + 1)
                w = min(4, TT - 4 * n) * P
                nc.scalar.activation(x2_h[:, 512 * n:512 * n + w], scores_ps[:, n // 2, n % 2, 0:w],
                                     ACT.Copy).then_inc(x2_h_ready, 1)
            act.wait_ge(gate_step, 3)
            nc.scalar.activation(lexp[:], logit[:], ACT.Exp).then_inc(ln_act, 1)

            with act.Fori(0, CH) as n:
                for u in range(NE * SL):
                    act.wait_ge(hidden_done, 32 * n + u + 1)
                    if u >= 3:
                        act.wait_ge(gated_done, 32 * n + u - 2)
                    nc.scalar.activation(gelu[:, u % 3, :], scores_ps[:, (u % 4) // 2, u % 2, 0:HALF], ACT.Gelu,
                                         bias=b1_c[:, u:u + 1]).then_inc(gelu_done, 1)
                act.wait_ge(summed, 32 * n + 32)
                nc.scalar.activation(xnT[:, bass.ds(n * HALF, HALF)], pv_ps[:, 0:HALF],
                                     ACT.Copy).then_inc(sum_copied, 1)

        @block.vector
        def _(dve):
            def norm(n):
                nc.vector.reduce_sum(ln_sum[:], tok[:], AX_X).then_inc(ln_step, 1)
                dve.wait_ge(ln_step, 8 * n + 1)
                nc.vector.tensor_scalar(ln_mean[:], ln_sum[:], 1.0 / D, None, ALU.mult).then_inc(ln_step, 1)
                dve.wait_ge(ln_step, 8 * n + 2)
                nc.vector.tensor_tensor(tok_c[:], tok[:],
                                        ln_mean[:].rearrange("p (t a) -> p t a", a=1).to_broadcast([P, TT, D]),
                                        ALU.subtract).then_inc(ln_step, 1)
                dve.wait_ge(ln_act, 2 * n + 1)
                nc.vector.reduce_sum(ln_sq[:], squares, AX_X).then_inc(ln_step, 1)
                dve.wait_ge(ln_step, 8 * n + 4)
                nc.vector.tensor_scalar(ln_var[:], ln_sq[:], 1.0 / D, LN_EPS, ALU.mult, ALU.add).then_inc(ln_step, 1)
                dve.wait_ge(ln_act, 2 * n + 2)
                nc.vector.reciprocal(ln_rstd[:], ln_std[:]).then_inc(ln_step, 1)
                dve.wait_ge(ln_step, 8 * n + 6)
                for half in (slice(0, 8), slice(8, TT)):
                    w = half.stop - half.start
                    nc.vector.tensor_tensor(tok_c[:, half], tok_c[:, half],
                                            ln_rstd[:, half].rearrange("p (t a) -> p t a", a=1).to_broadcast([P, w, D]),
                                            ALU.mult).then_inc(ln_step, 1)

            nc.vector.memset(wk_rows[0:1, :], 0.0)
            nc.vector.memset(wv_rows[0:1, :], 0.0).then_inc(weights_split, 1)
            dve.wait_ge(tok_loaded, 16)
            norm(0)
            dve.wait_ge(small_loaded, SMALL * 16)
            dve.wait_ge(weights_split, 1)
            nc.vector.tensor_copy(wv_h[:], wv_rows[:]).then_inc(weights_split, 1)
            nc.vector.tensor_copy(wg_h[:], wg[:]).then_inc(weights_split, 1)
            nc.vector.tensor_copy(b2_h[:], b2_r[:]).then_inc(weights_split, 1)
            dve.wait_ge(weights_split, 4)
            nc.vector.tensor_tensor(b2_l[:], b2_r[:], b2_h[:].bitcast(F32), ALU.subtract).then_inc(weights_split, 1)
            nc.vector.tensor_tensor(wv_l[:], wv_rows[:], wv_h[:].bitcast(F32), ALU.subtract).then_inc(weights_split, 1)
            nc.vector.tensor_tensor(wg_l[:], wg[:], wg_h[:].bitcast(F32), ALU.subtract).then_inc(weights_split, 1)
            dve.wait_ge(tanh_ready, 1)
            nc.vector.tensor_scalar(bo_gated[:], bo_b[:], gate_tanh[0:NQ, 0:1], None, ALU.mult).then_inc(bo_ready, 1)
            dve.wait_ge(consts_ready, 6)
            nc.vector.tensor_copy(expert_pick[:], pick_f[:]).then_inc(weights_split, 1)

            def ctx_low(b, k, g):
                dve.wait_ge(ctx_h_ready, NG * b + g + 1)
                nc.vector.tensor_tensor(ctx_l[k][:, GT * g:GT * g + GT, :],
                                        prep_ps[0:CR, g % 2, 0:GT * KP].rearrange("c (t p) -> c t p", p=KP),
                                        ctx_h[k][:, GT * g:GT * g + GT, :].bitcast(F32),
                                        ALU.subtract).then_inc(ctx_l_ready, 1)

            def q_low(b, k, n):
                dve.wait_ge(q_h_ready, 2 * b + n + 1)
                nc.vector.tensor_tensor(q_l[k][:, n * HALF:(n + 1) * HALF], prep_ps[0:CR, 1 - n, 0:HALF],
                                        q_h[k][:, n * HALF:(n + 1) * HALF].bitcast(F32),
                                        ALU.subtract).then_inc(q_l_ready, 1)

            def values(b, k, g):
                dve.wait_ge(val_done, NG * b + g + 1)
                nc.vector.tensor_copy(val[k][:, GT * g:GT * g + GT, :, 0:2 * HD],
                                      misc_ps[0:KP, :].rearrange("k (t p d) -> k t p d", t=GT, d=2 * HD)
                                      ).then_inc(val_copied, 1)

            def reduce_tile(b, j):
                for c in range(MC):
                    n = MC * j + c
                    dve.wait_ge(max_scored, MT * MC * b + n + 1)
                    nc.vector.reduce_max(part_max[:, j, c:c + 1], prep_ps[:, (n + 1) % 2, 0:CK],
                                         AX_X).then_inc(max_reduced, 1)

            def negate_max(b):
                dve.wait_ge(max_reduced, MT * MC * (b + 1))
                nc.vector.tensor_reduce(neg_max[:], part_max[:], AX_X, ALU.max, negate=True).then_inc(neg_max_ready, 1)

            def copy_row(b, k):
                dve.wait_ge(max_row_done, b + 1)
                nc.vector.tensor_copy(q_h[k][0:1, 0:512], prep_ps[0:1, 0, :]).then_inc(max_row_copied, 1)
                nc.vector.tensor_copy(q_h[k][0:1, 512:HQ], prep_ps[0:1, 1, 0:HQ - 512]).then_inc(max_row_copied, 1)

            def normalise(b):
                v = misc_ps[0:NQ, :].rearrange("q (r a j w) -> q r a j w", r=R, a=2, j=J)
                dve.wait_ge(acc_transposed, b + 1)
                nc.vector.reciprocal(den_inv[:].rearrange("q (n a) -> q n a", a=1),
                                     misc_ps[0:NQ, :].rearrange("q (n w) -> q n w", w=VW)[:, :, 2 * HD:2 * HD + 1]
                                     ).then_inc(den_ready, 1)
                dve.wait_ge(den_ready, b + 1)
                for a in range(2):
                    for r in range(R):
                        o = heads[:].rearrange("q (r j a d) -> q r a j d", r=R, j=J, a=2)[:, r, a]
                        d = den_inv[:].rearrange("q (r a j w) -> q r a j w", r=R, a=2, w=1)[:, r, a]
                        ins = nc.vector.tensor_tensor(o, v[:, r, a, :, HD * a:HD * a + HD],
                                                      d.to_broadcast([NQ, J, HD]), ALU.mult)
                ins.then_inc(heads_ready, 1)

            def residual(b, k):
                dve.wait_ge(projected, b + 1)
                dve.wait_ge(x_bo_ready, b + 1)
                nc.vector.scalar_tensor_tensor(out=x1[k][:], in0=misc_ps[0:NQ, 0:D], scalar=gate_tanh[0:NQ, 0:1],
                                               in1=x_bo[k][:], op0=ALU.mult, op1=ALU.add).then_inc(x1_ready, 1)

            for g in range(NG):
                ctx_low(0, 0, g)
            for n in range(2):
                q_low(0, 0, n)
            for j in range(MT):
                if j < NG:
                    values(0, 0, j)
                reduce_tile(0, j)
            negate_max(0)
            copy_row(0, 0)

            def main(b, k, first, last):
                for t in range(KT):
                    if not last:
                        c, m = b + 1, 1 - k
                        if t == 0:
                            ctx_low(c, m, 0)
                            ctx_low(c, m, 1)
                        if t == 1:
                            ctx_low(c, m, 2)
                        if t in (2, 3):
                            q_low(c, m, t - 2)
                        if 4 <= t <= 10:
                            reduce_tile(c, t - 4)
                    if not first:
                        if t == 2:
                            normalise(b - 1)
                        if t == 4:
                            residual(b - 1, 1 - k)
                    if not last and 5 <= t <= 7:
                        values(c, m, t - 5)
                if not last:
                    negate_max(b + 1)
                    copy_row(b + 1, 1 - k)

            batches(dve, main)
            normalise(B - 1)
            residual(B - 1, 1)

            dve.wait_ge(x1_loaded, 16)
            norm(1)
            for n in range(4):
                dve.wait_ge(x2_h_ready, n + 1)
                w = min(4, TT - 4 * n) * P
                nc.vector.tensor_tensor(x2_l[:, 512 * n:512 * n + w], scores_ps[:, n // 2, n % 2, 0:w],
                                        x2_h[:, 512 * n:512 * n + w].bitcast(F32), ALU.subtract).then_inc(x2_l_ready, 1)

            steps = [0]

            def step(ins):
                steps[0] += 1
                ins.then_inc(gate_step, 1)
                dve.wait_ge(gate_step, steps[0])

            def over_experts(v):
                return v.rearrange("p (t a) -> p t a", a=1).to_broadcast([P, TT, NE])

            dve.wait_ge(logits_done, 1)
            step(nc.vector.tensor_tensor(logit[:], misc_ps[:, 0:TT * NE].rearrange("p (t e) -> p t e", e=NE),
                                         bg_b[:].rearrange("p (a e) -> p a e", a=1).to_broadcast([P, TT, NE]),
                                         ALU.add))
            step(nc.vector.reduce_max(lmax[:], logit[:], AX_X))
            step(nc.vector.tensor_tensor(logit[:], logit[:], over_experts(lmax[:]), ALU.subtract))
            dve.wait_ge(ln_act, 5)
            step(nc.vector.reduce_sum(lsum[:], lexp[:], AX_X))
            step(nc.vector.reciprocal(lmax[:], lsum[:]))
            step(nc.vector.tensor_tensor(gates[:], lexp[:], over_experts(lmax[:]), ALU.mult))
            other = gates[:].rearrange("p t (a f) -> p t a f", a=1).to_broadcast([P, TT, NE, NE])
            mine = gates[:].rearrange("p t (e a) -> p t e a", a=1).to_broadcast([P, TT, NE, NE])
            gt = cmp_gt.rearrange("p t (e f) -> p t e f", f=NE)
            eq = cmp_eq.rearrange("p t (e f) -> p t e f", f=NE)
            step(nc.vector.tensor_tensor(gt, other, mine, ALU.is_gt))
            step(nc.vector.tensor_tensor(eq, other, mine, ALU.is_equal))
            step(nc.vector.tensor_tensor(cmp_eq, cmp_eq,
                                         lower[:].rearrange("p e f -> p (e f)").rearrange("p (a n) -> p a n", a=1).to_broadcast([P, TT, NE * NE]),
                                         ALU.mult))
            step(nc.vector.tensor_tensor(cmp_gt, cmp_gt, cmp_eq, ALU.add))
            step(nc.vector.reduce_sum(rank[:], gt, AX_X))
            step(nc.vector.tensor_scalar(rank[:], rank[:], TOP - 0.5, None, ALU.is_lt))
            step(nc.vector.tensor_tensor(gates[:], gates[:], rank[:], ALU.mult))
            step(nc.vector.reduce_sum(lsum[:], gates[:], AX_X))
            step(nc.vector.tensor_scalar(lsum[:], lsum[:], GATE_EPS, None, ALU.max))
            step(nc.vector.reciprocal(lmax[:], lsum[:]))
            step(nc.vector.tensor_tensor(gates[:], gates[:], over_experts(lmax[:]), ALU.mult))
            step(nc.vector.tensor_copy(gate_hl[:, :, 0:NE], gates[:]))
            step(nc.vector.tensor_tensor(gate_hl[:, :, NE:2 * NE], gates[:], gate_hl[:, :, 0:NE].bitcast(F32),
                                         ALU.subtract))
            for n in range(4):
                w = min(4, TT - 4 * n) * P
                cols = slice(512 * n, 512 * n + w)
                dve.wait_ge(gates_transposed, n + 1)
                nc.vector.tensor_copy(gT2[:, cols], prep_ps[0:2 * NE, n % 2, 0:w]).then_inc(gates_copied, 1)

            with dve.Fori(0, CH) as n:
                for u in range(NE * SL):
                    dve.wait_ge(gelu_done, 32 * n + u + 1)
                    if u % SL == 0:
                        dve.wait_ge(spread_done, NE * n + u // SL + 1)
                    if u >= 3:
                        dve.wait_ge(summed, 32 * n + u - 2)
                    nc.vector.tensor_tensor(gated[:, u % 3, :], prep_ps[:, (u // SL) % 2, 0:HALF], gelu[:, u % 3, :],
                                            ALU.mult).then_inc(gated_done, 1)
            for n in range(4):
                dve.wait_ge(y_transposed, n + 1)
                w = min(4, TT - 4 * n)
                nc.vector.scalar_tensor_tensor(
                    out=y_sb[:, 4 * n:4 * n + w, :].rearrange("p t d -> p (t d)"),
                    in0=scores_ps[:, n // 2, n % 2, 0:w * P], scalar=gate_tanh[:, 1:2],
                    in1=tok[:, 4 * n:4 * n + w, :].rearrange("p t d -> p (t d)"),
                    op0=ALU.mult, op1=ALU.add).then_inc(y_ready, 1)

        @block.tensor
        def _(pe):
            mm = nc.tensor.matmul

            def transpose_tokens(n0):
                for n in range(4):
                    w = min(4, TT - 4 * n)
                    pe.wait_ge(ln_step, 8 * n0 + (7 if n < 2 else 8))
                    for t in range(4 * n, 4 * n + w):
                        last = nc.tensor.transpose(scores_ps[:, n // 2, n % 2, (t % 4) * P:(t % 4 + 1) * P],
                                                   tok_c[:, t, :], ident[:])
                    last.then_inc(xn_transposed, 1)

            pe.wait_ge(consts_ready, 1)
            pe.wait_ge(small_loaded, SMALL * 16)
            pe.wait_ge(weights_split, 1)
            nc.tensor.transpose(misc_ps[:, 0:CR], wk_rows[:], ident[0:CR, 0:CR])
            nc.tensor.transpose(misc_ps[:, P:P + NE * SL], b1_rows[:], ident[0:NE * SL, 0:NE * SL]
                                ).then_inc(wk_transposed, 1)
            transpose_tokens(0)
            pe.wait_ge(xn_copied, 4)
            for n in range(CH):
                mm(scores_ps[:, n // 2, n % 2, 0:HALF], wq[:], xnT[:, n * HALF:(n + 1) * HALF],
                   start=True, stop=True).then_inc(q_projected, 1)
            pe.wait_ge(wk_copied, 1)
            pe.wait_ge(weights_split, 8)
            pe.wait_ge(frames_ready, 4)

            def ctx_transpose(b, k, g, first):
                if g == 0:
                    pe.wait_ge(nat_loaded[k], 16 * (b // 2) + 16 if isinstance(b, int) else 8 * (b - k) + 16)
                    if not first:
                        pe.wait_ge(max_row_copied, 2 * b)
                if g == 2:
                    pe.wait_ge(ctx_l_ready, NG * b + 1)
                for t in range(GT):
                    last = nc.tensor.transpose(prep_ps[0:CR, g % 2, t * KP:(t + 1) * KP],
                                               nat[k][:, GT * g + t, :], ident[0:KP, 0:KP])
                last.then_inc(ctx_transposed, 1)

            def fold_queries(b, n):
                if n == 0:
                    pe.wait_ge(q_diag_ready, b + 1)
                pe.wait_ge(ctx_l_ready, NG * b + 2 + n)
                mm(prep_ps[0:CR, 1 - n, 0:HALF], wk_fold[:],
                   q_diag[:].rearrange("p h q -> p (h q)")[:, n * HALF:(n + 1) * HALF],
                   start=True, stop=True).then_inc(q_folded, 1)

            def make_values(b, k, g):
                if g == 0:
                    pe.wait_ge(x1_ready, b - 1) if not (isinstance(b, int) and b < 2) else None
                else:
                    pe.wait_ge(val_copied, NG * b + g)
                for t in range(GT):
                    o = misc_ps[0:KP, t * D:(t + 1) * D]
                    mm(o, ctx_h[k][:, GT * g + t, :], wv_h[:], start=True, stop=False)
                    mm(o, ctx_h[k][:, GT * g + t, :], wv_l[:], start=False, stop=False)
                    last = mm(o, ctx_l[k][:, GT * g + t, :], wv_h[:], start=False, stop=True)
                last.then_inc(val_done, 1)

            def max_chunk(b, k, n):
                j, c = n // MC, n % MC
                if n < 2:
                    pe.wait_ge(q_l_ready, 2 * b + n + 1)
                    if n == 0:
                        pe.wait_ge(q_h_ready, 2 * b + 2)
                else:
                    pe.wait_ge(max_reduced, MT * MC * b + n - 1)
                mm(prep_ps[:, (n + 1) % 2, 0:CK], q_h[k][:, j * P:(j + 1) * P],
                   ctx_h[k][:].rearrange("c t p -> c (t p)")[:, c * CK:(c + 1) * CK],
                   start=True, stop=True).then_inc(max_scored, 1)

            def max_row(b):
                pe.wait_ge(neg_max_ready, b + 1)
                for j in range(MT):
                    last = nc.tensor.transpose(prep_ps[0:1, j // 4, (j % 4) * P:(j % 4 + 1) * P],
                                               neg_max[:, j:j + 1], ident[:])
                last.then_inc(max_row_done, 1)

            def score_half(b, k, t, n, first):
                if t == 0 and n == 0:
                    pe.wait_ge(max_row_copied, 2 * b + 2)
                    pe.wait_ge(q_l_ready, 2 * b + 2)
                if n == 0 and not (first and t < 2):
                    pe.wait_ge(exp_done, KT * b + t - 1)
                o = scores_ps[0:KP, t % 2, n, 0:HALF]
                cols = slice(n * HALF, (n + 1) * HALF)
                mm(o, ctx_h[k][:, t, :], q_h[k][:, cols], start=True, stop=False)
                mm(o, ctx_h[k][:, t, :], q_l[k][:, cols], start=False, stop=False)
                last = mm(o, ctx_l[k][:, t, :], q_h[k][:, cols], start=False, stop=True)
                if n == 1:
                    last.then_inc(scored, 1)

            def value_tile(b, k, t, first):
                pe.wait_ge(exp_done, KT * b + t + 1)
                if t == 0:
                    pe.wait_ge(val_copied, NG * b + NG)
                    if not first:
                        pe.wait_ge(acc_copied, b)
                for r in range(R):
                    for j in range(J):
                        p = J * r + j
                        last = mm(pv_ps[VW * j:VW * j + VW, r * PQ:(r + 1) * PQ], val[k][:, t, p, :],
                                  prob[t % 2][:, p * PQ:(p + 1) * PQ], start=(t == 0 and r == 0), stop=(t == KT - 1),
                                  skip_group_check=True)
                last.then_inc(pv_done, 1)

            def await_acc(b, last_batch):
                pe.wait_ge(acc_copied, b + 1)
                if last_batch:
                    pe.wait_ge(x1_ready, b)
                else:
                    pe.wait_ge(val_copied, NG * b + NG + NG)

            def transpose_acc(b):
                for r in range(R):
                    for a in range(2):
                        n = 2 * r + a
                        last = nc.tensor.transpose(misc_ps[0:NQ, n * P:(n + 1) * P], acc[:, r, a, :], ident[:])
                last.then_inc(acc_transposed, 1)

            def transpose_heads(b):
                nc.tensor.transpose(misc_ps[:, 0:NQ], heads[:], ident[0:NQ, 0:NQ]).then_inc(heads_transposed, 1)

            def project(b):
                pe.wait_ge(headsT_copied, b + 1)
                mm(misc_ps[0:NQ, 0:D], headsT[:], wo[:], start=True, stop=True).then_inc(projected, 1)

            for g in range(NG):
                ctx_transpose(0, 0, g, True)
            for n in range(2):
                fold_queries(0, n)
            for j in range(MT):
                if j < NG:
                    make_values(0, 0, j)
                for c in range(MC):
                    max_chunk(0, 0, MC * j + c)
            max_row(0)

            def main(b, k, first, last):
                c, m = b + 1, 1 - k
                for t in range(KT):
                    if t == 0 and not first:
                        value_tile(b - 1, m, KT - 1, False)
                    maxima = not last and 4 <= t <= 10
                    score_half(b, k, t, 0, first)
                    if maxima:
                        max_chunk(c, m, MC * (t - 4))
                    score_half(b, k, t, 1, first)
                    if maxima:
                        max_chunk(c, m, MC * (t - 4) + 1)
                    if t == 2 and not first:
                        await_acc(b - 1, False)
                    if t == 3 and not first:
                        pe.wait_ge(heads_ready, b)
                    if not last:
                        if t == 0:
                            ctx_transpose(c, m, 0, False)
                            ctx_transpose(c, m, 1, False)
                        if t == 1:
                            ctx_transpose(c, m, 2, False)
                        if t in (2, 3):
                            fold_queries(c, t - 2)
                    if not first:
                        if t == 2:
                            transpose_acc(b - 1)
                        if t == 3:
                            transpose_heads(b - 1)
                        if t == 4:
                            project(b - 1)
                    if not last:
                        if 5 <= t <= 7:
                            make_values(c, m, t - 5)
                        if t == KT - 1:
                            max_row(c)
                    if t >= 1:
                        value_tile(b, k, t - 1, first)
                    if maxima:
                        max_chunk(c, m, MC * (t - 4) + 2)

            batches(pe, main)
            value_tile(B - 1, 1, KT - 1, False)
            await_acc(B - 1, True)
            transpose_acc(B - 1)
            pe.wait_ge(heads_ready, B)
            transpose_heads(B - 1)
            project(B - 1)

            transpose_tokens(1)
            pe.wait_ge(x1_ready, B)
            for t in range(TT):
                pe.wait_ge(x2_l_ready, t // 4 + 1)
                o = misc_ps[:, t * NE:(t + 1) * NE]
                mm(o, x2_h[:, t * P:(t + 1) * P], wg_h[:], start=True, stop=False)
                mm(o, x2_h[:, t * P:(t + 1) * P], wg_l[:], start=False, stop=False)
                last = mm(o, x2_l[:, t * P:(t + 1) * P], wg_h[:], start=False, stop=True)
            last.then_inc(logits_done, 1)
            pe.wait_ge(gate_step, GATE_STEPS)
            for n in range(4):
                if n >= 2:
                    pe.wait_ge(gates_copied, n - 1)
                w = min(4, TT - 4 * n)
                for t in range(4 * n, 4 * n + w):
                    last = nc.tensor.transpose(prep_ps[0:2 * NE, n % 2, (t % 4) * P:(t % 4 + 1) * P],
                                               gate_hl[:, t, :].bitcast(F32), ident[:])
                last.then_inc(gates_transposed, 1)
            pe.wait_ge(gates_copied, 4)
            pe.wait_ge(w1_split, NE)
            pe.wait_ge(w2_loaded, 16)

            with pe.Fori(0, CH) as n:
                tokens = bass.ds(n * HALF, HALF)

                def hidden(u):
                    e, s = u // SL, u % SL
                    o = scores_ps[:, (u % 4) // 2, u % 2, 0:HALF]
                    wh = w1_h[:, e, s * P:(s + 1) * P]
                    mm(o, wh, x2_h[:, tokens], start=True, stop=False)
                    mm(o, wh, x2_l[:, tokens], start=False, stop=False)
                    mm(o, w1_l[:, e, s * P:(s + 1) * P], x2_h[:, tokens], start=False, stop=True
                       ).then_inc(hidden_done, 1)

                def accumulate(u):
                    mm(pv_ps[:, 0:HALF], w2[:, u, :], gated[:, u % 3, :], start=False, stop=(u == NE * SL - 1)
                       ).then_inc(summed, 1)

                for u in range(NE * SL):
                    if u >= 4:
                        pe.wait_ge(gelu_done, 32 * n + u - 3)
                    if u % SL == 0 and u >= 2 * SL:
                        pe.wait_ge(gated_done, 32 * n + u - SL)
                    if u == 2:
                        pe.wait_ge(gelu_done, 32 * n + 1)
                    hidden(u)
                    if u % SL == 0:
                        e = u // SL
                        mm(prep_ps[:, e % 2, 0:HALF], expert_pick[:, e, :], gT2[:, tokens],
                           start=True, stop=True).then_inc(spread_done, 1)
                    if u == 2:
                        mm(pv_ps[:, 0:HALF], b2_h[:], gT2[:, tokens], start=True, stop=False)
                        mm(pv_ps[:, 0:HALF], b2_l[:], gT2[:, tokens], start=False, stop=False)
                    if u >= 2:
                        pe.wait_ge(gated_done, 32 * n + u - 1)
                        accumulate(u - 2)
                for u in (NE * SL - 2, NE * SL - 1):
                    pe.wait_ge(gated_done, 32 * n + u + 1)
                    accumulate(u)

            pe.wait_ge(sum_copied, CH)
            for n in range(4):
                w = min(4, TT - 4 * n)
                for t in range(4 * n, 4 * n + w):
                    last = nc.tensor.transpose(scores_ps[:, n // 2, n % 2, (t % 4) * P:(t % 4 + 1) * P],
                                               xnT[:, t * P:(t + 1) * P], ident[:])
                last.then_inc(y_transposed, 1)


_INS = ['x', 'ctx_768', 'g_xattn', 'g_ffn', 'L0_xattn_Wq', 'L0_xattn_bq', 'L0_xattn_Wk', 'L0_xattn_bk',
        'L0_xattn_Wv', 'L0_xattn_bv', 'L0_xattn_Wo', 'L0_xattn_bo', 'L0_ffn_Wg', 'L0_ffn_bg', 'L0_ffn_W1',
        'L0_ffn_b1', 'L0_ffn_W2', 'L0_ffn_b2']
_OUT = ((32, 56, 128), 'float32')


def kernel(**inputs):
    import numpy as _np
    import concourse.bacc as _bacc
    from concourse import mybir as _mybir
    from concourse.bass_utils import run_bass_kernel_spmd as _run

    nc = _bacc.Bacc("TRN2", target_bir_lowering=False, num_devices=1)
    arrays, args = {}, []
    for name in _INS:
        a = _np.ascontiguousarray(inputs[name])
        arrays[f"in_{name}_dram"] = a
        args.append(nc.dram_tensor(f"in_{name}_dram", a.shape, _mybir.dt.from_np(a.dtype), kind="ExternalInput").ap())
    shape, dtype = _OUT
    out = nc.dram_tensor("out_0_dram", shape, _mybir.dt.from_np(_np.dtype(dtype)), kind="ExternalOutput").ap()
    gated_xattn_moe(nc, *args, out)
    r = _run(nc, [arrays], core_ids=[0])
    return r.results[0]["out_0_dram"]
```

```python
from contextlib import ExitStack

import concourse.bass as bass
from concourse import mybir

F32 = mybir.dt.float32
F32R = mybir.dt.float32r
ALU = mybir.AluOpType
ACT = mybir.ActivationFunctionType
AX_X = mybir.AxisListType.X

P = 128


def gated_xattn_moe(nc, x, ctx, g_xattn, g_ffn, Wq, bq, Wk, bk, Wv, bv, Wo, bo,
                    Wg, bg, W1, b1, W2, b2, out):
    B, NQ, D = x.shape
    _, NK, KD = ctx.shape
    HEADS = 16
    HD = D // HEADS
    SCALE = float(HD) ** -0.5
    LN_EPS, GATE_EPS = 1e-5, 1e-12
    KT = 12
    KP = NK // KT
    HQ = HEADS * NQ
    HALF = HQ // 2
    SIDE = P // 2
    CR = KD + 1
    GT = 4
    NG = KT // GT
    CK = GT * KP
    MT = HQ // P
    MN = MT * NG
    PAIRS = HEADS // 2
    PQ = 2 * NQ
    VW = 32
    J, R = 4, 2
    TOK = B * NQ
    TT = TOK // P
    NE, HID = W1.shape[0], W1.shape[2]
    SL = HID // P
    NU = NE * SL
    CH = TOK // HALF
    TOP = 2
    VALUE_STEPS = (0, 5, 6)
    GATE_STEPS = 19
    EARLY_LOADS, LATE_LOADS = 6, 9
    assert KT * KP == NK and MT * P == HQ and TT * P == TOK and CH * HALF == TOK and D == P

    with ExitStack() as stack:
        def sb(name, shape, dt=F32):
            return stack.enter_context(nc.sbuf_tensor(name, shape, dt))

        def psum(name, shape):
            return stack.enter_context(nc.psum_tensor(name, shape, F32))

        def sem(name):
            return stack.enter_context(nc.semaphore(name))

        x1_dram = nc.dram_tensor("x1_scratch", [TOK, D], F32, kind="Internal").ap()

        scores_ps = psum("scores_ps", [P, 2, 2, 512])
        prep_ps = psum("prep_ps", [P, 2, 512])
        pv_ps = psum("pv_ps", [P, 512])
        misc_ps = psum("misc_ps", [P, 512])

        ident = sb("ident", [P, P])
        head_mask = sb("head_mask", [P, HEADS])
        side_mask = sb("side_mask", [P, HEADS // 2])
        minus_half = sb("minus_half", [NQ, 1])
        ln_eps_c = sb("ln_eps_c", [NQ, 1])
        wq = sb("wq", [P, 2, D])
        bq_c = sb("bq_c", [P, 2])
        wk_rows = sb("wk_rows", [CR, D])
        wv_rows = sb("wv_rows", [CR, D])
        wo = sb("wo", [P, D])
        gate_in = sb("gate_in", [P, 2])
        gate_tanh = sb("gate_tanh", [P, 2])
        bo_b = sb("bo_b", [NQ, D])
        bo_gated = sb("bo_gated", [NQ, D])
        wg = sb("wg", [P, NE])
        wg_h = sb("wg_h", [P, NE], F32R)
        wg_l = sb("wg_l", [P, NE], F32R)
        bg_b = sb("bg_b", [P, NE])
        w1 = sb("w1", [P, NE, HID])
        b1_rows = sb("b1_rows", [NU, P])
        b1_c = sb("b1_c", [P, NU])
        w2 = sb("w2", [P, NU, D])
        b2_r = sb("b2_r", [2 * NE, D])
        b2_h = sb("b2_h", [2 * NE, D], F32R)
        b2_l = sb("b2_l", [2 * NE, D], F32R)
        lower = sb("lower", [P, NE, NE])
        expert_pick = sb("expert_pick", [2 * NE, NE, P], F32R)

        nat = [sb(f"nat{k}", [KP, KT, CR]) for k in range(2)]
        ctxT = sb("ctxT", [CR, KT, KP])
        key_h = sb("key_h", [P, KT, KP], F32R)
        key_l = sb("key_l", [P, KT, KP], F32R)
        maxT = sb("maxT", [MT, P], F32R)
        keys = sb("keys", [P, 2, 2, 2, KT, KP], F32R)
        key_hl = [[keys[:, k, 0, n] for n in range(2)] for k in range(2)]
        key_h1 = [[keys[:, k, 1, n] for n in range(2)] for k in range(2)]
        q_h = [sb(f"q_h{k}", [P, HEADS, NQ], F32R) for k in range(2)]
        q_lh = [sb(f"q_lh{k}", [P, 2, HEADS // 2, NQ], F32R) for k in range(2)]
        q_full = sb("q_full", [P, NQ])
        q_round = sb("q_round", [P, NQ], F32R)
        q_pair = sb("q_pair", [P, 2, NQ])
        val_all = sb("val_all", [P, 2, KT, PAIRS, VW])
        val = [val_all[0:KP, k] for k in range(2)]
        prob = [sb(f"prob{k}", [KP, HQ]) for k in range(2)]
        x_res = [sb(f"x_res{k}", [NQ, D]) for k in range(2)]
        x_bo = [sb(f"x_bo{k}", [NQ, D]) for k in range(2)]
        x1 = [sb(f"x1_{k}", [NQ, D]) for k in range(2)]
        xn = sb("xn", [NQ, D])
        xnT = sb("xnT", [P, NQ])
        stats = [sb(f"stats{n}", [NQ, 6]) for n in range(2)]
        mean_var = [sb(f"mean_var{n}", [NQ, 2]) for n in range(2)]
        var_eps = [sb(f"var_eps{n}", [NQ, 1]) for n in range(2)]
        rstd = [sb(f"rstd{n}", [NQ, 1]) for n in range(2)]
        xn2 = sb("xn2", [NQ, D])
        part_max = sb("part_max", [P, MT, NG])
        neg_max = sb("neg_max", [P, MT])
        acc = sb("acc", [P, R, 2, NQ])
        den_inv = sb("den_inv", [NQ, HEADS])
        heads = sb("heads", [NQ, D])
        headsT = sb("headsT", [P, NQ])

        x2_h = sb("x2_h", [P, TOK], F32R)
        x2_l = sb("x2_l", [P, TOK], F32R)
        keys_flat = keys[:].rearrange("p a b c t n -> p (a b c t n)")
        w1_h = keys_flat[:, 0:NE * HID].rearrange("p (e h) -> p e h", e=NE)
        w1_l = keys_flat[:, NE * HID:2 * NE * HID].rearrange("p (e h) -> p e h", e=NE)
        tok = sb("tok", [P, TT, D])
        sumT = sb("sumT", [P, TOK])
        gT2 = sb("gT2", [2 * NE, TOK], F32R)
        logit = sb("logit", [P, TT, NE])
        lmax = sb("lmax", [P, TT])
        lexp = sb("lexp", [P, TT, NE])
        lsum = sb("lsum", [P, TT])
        gates = sb("gates", [P, TT, NE])
        rank = sb("rank", [P, TT, NE])
        cmp_gt = sumT[:, 0:HALF * 2].rearrange("p (t n) -> p t n", t=TT)
        cmp_eq = sumT[:, HALF * 2:].rearrange("p (t n) -> p t n", t=TT)
        gate_hl = key_h[:].rearrange("p t n -> p (t n)")[:, 0:TT * 2 * NE].rearrange("p (t e) -> p t e", t=TT)
        gelu, gated = (val_all[:, k].rearrange("p t a d -> p (t a d)")[:, 0:3 * HALF]
                       .rearrange("p (n q) -> p n q", n=3) for k in range(2))

        early_loaded = sem("early_loaded")
        late_loaded = sem("late_loaded")
        w_loaded = sem("w_loaded")
        nat_loaded = [sem(f"nat_loaded{k}") for k in range(2)]
        x_res_loaded = [sem(f"x_res_loaded{k}") for k in range(2)]
        x1_stored = [sem(f"x1_stored{k}") for k in range(2)]
        x1_loaded = sem("x1_loaded")
        out_stored = sem("out_stored")
        blanks_ready = sem("blanks_ready")
        consts_ready = sem("consts_ready")
        ones_ready = sem("ones_ready")
        tanh_ready = sem("tanh_ready")
        weights_split = sem("weights_split")
        wq_ready = sem("wq_ready")
        bo_ready = sem("bo_ready")
        b1_transposed = sem("b1_transposed")
        ln_stats = [sem(f"ln{n}_stats") for n in (1, 2)]
        ln_var = [sem(f"ln{n}_var") for n in (1, 2)]
        ln_eps = [sem(f"ln{n}_eps") for n in (1, 2)]
        ln_rstd = [sem(f"ln{n}_rstd") for n in (1, 2)]
        ln_done = [sem(f"ln{n}_done") for n in (1, 2)]
        xn_transposed = sem("xn_transposed")
        xnT_copied = sem("xnT_copied")
        q_projected = sem("q_projected")
        q_copied = sem("q_copied")
        q_rounded = sem("q_rounded")
        q_split = sem("q_split")
        q_h_ready = sem("q_h_ready")
        q_lh_ready = sem("q_lh_ready")
        ctx_transposed = sem("ctx_transposed")
        ctx_copied = sem("ctx_copied")
        k_projected = sem("k_projected")
        k_h_ready = sem("k_h_ready")
        k_l_ready = sem("k_l_ready")
        k_copied = sem("k_copied")
        max_scored = sem("max_scored")
        max_reduced = sem("max_reduced")
        neg_max_ready = sem("neg_max_ready")
        max_transposed = sem("max_transposed")
        maxT_ready = sem("maxT_ready")
        max_placed = sem("max_placed")
        val_done = sem("val_done")
        val_copied = sem("val_copied")
        scored = sem("scored")
        exp_done = sem("exp_done")
        pv_done = sem("pv_done")
        acc_copied = sem("acc_copied")
        acc_transposed = sem("acc_transposed")
        den_ready = sem("den_ready")
        heads_ready = sem("heads_ready")
        heads_transposed = sem("heads_transposed")
        headsT_copied = sem("headsT_copied")
        projected = sem("projected")
        x_bo_ready = sem("x_bo_ready")
        x1_ready = sem("x1_ready")
        x2_transposed = sem("x2_transposed")
        x2_h_ready = sem("x2_h_ready")
        x2_l_ready = sem("x2_l_ready")
        w1_h_ready = sem("w1_h_ready")
        w1_split = sem("w1_split")
        logits_done = sem("logits_done")
        gate_step = sem("gate_step")
        gate_exp = sem("gate_exp")
        gates_transposed = sem("gates_transposed")
        gates_copied = sem("gates_copied")
        hidden_done = sem("hidden_done")
        gelu_done = sem("gelu_done")
        spread_done = sem("spread_done")
        gated_done = sem("gated_done")
        summed = sem("summed")
        sum_copied = sem("sum_copied")
        y_transposed = sem("y_transposed")
        y_ready = sem("y_ready")

        ctx_v = ctx.rearrange("b (p t) c -> b p t c", t=KT)
        x1_b = x1_dram.rearrange("(b q) d -> b q d", q=NQ)
        x1_tok = x1_dram.rearrange("(t p) d -> p t d", p=P)
        out_tok = out.rearrange("b q d -> (b q) d").rearrange("(t p) d -> p t d", p=P)

        def row(v):
            return v.rearrange("(a n) -> a n", a=1)

        def column(v):
            return v.rearrange("(p a) -> p a", a=1)

        def batches(engine, main):
            main(0, 0, 2)
            with engine.Fori(0, (B - 4) // 2) as i:
                main(2 * i + 1, 1, 2)
                main(2 * i + 2, 0, 2)
            for b in range(B - 3, B):
                main(b, b % 2, min(2, B - 1 - b))

        def is_first(b):
            return isinstance(b, int) and b == 0

        def uses(b, k):
            return 16 * (b // 2) + 16 if isinstance(b, int) else 8 * (b - k) + 16

        block = stack.enter_context(nc.Block())

        @block.sync
        def _(sp):
            sp.dma_start(x_res[0][:], x[0]).then_inc(x_res_loaded[0], 16)
            sp.dma_start(nat[0][:, :, 0:KD], ctx_v[0]).then_inc(nat_loaded[0], 16)
            sp.wait_ge(early_loaded, EARLY_LOADS * 16)
            sp.wait_ge(nat_loaded[0], 16)
            sp.dma_start(x_res[1][:], x[1]).then_inc(x_res_loaded[1], 16)
            sp.dma_start(nat[1][:, :, 0:KD], ctx_v[1]).then_inc(nat_loaded[1], 16)
            for dst, src in ((gate_in[:, 0:1], row(g_xattn).to_broadcast([P, 1])),
                             (gate_in[:, 1:2], row(g_ffn).to_broadcast([P, 1])),
                             (bo_b[:], row(bo).to_broadcast([NQ, D])),
                             (wo[:], Wo), (wg[:], Wg), (bg_b[:], row(bg).to_broadcast([P, NE])),
                             (b1_rows[:], b1.rearrange("e (s p) -> (e s) p", p=P)),
                             (b2_r[0:NE, :], b2), (b2_r[NE:2 * NE, :], b2)):
                sp.dma_start(dst, src).then_inc(late_loaded, 16)

            def load_ctx(b, k):
                sp.wait_ge(ctx_transposed, NG * b - NG)
                sp.dma_start(nat[k][:, :, 0:KD], ctx_v[b]).then_inc(nat_loaded[k], 16)

            def copy_keys(b, k):
                sp.wait_ge(k_l_ready, NG * b + NG)
                if not (isinstance(b, int) and b < 2):
                    sp.wait_ge(scored, KT * b - KT)
                halves = (slice(0, SIDE), slice(SIDE, P))
                for n in range(2):
                    sp.dma_start(keys[halves[n], k, :, n].bitcast(F32),
                                 key_h[halves[n]].bitcast(F32).rearrange("p (a t) n -> p a t n", a=1)
                                 .to_broadcast([SIDE, 2, KT, KP])).then_inc(k_copied, 16)
                    sp.dma_start(key_hl[k][n][halves[1 - n]].bitcast(F32), key_l[halves[n]].bitcast(F32)
                                 ).then_inc(k_copied, 16)

            def place_max(b, k):
                sp.wait_ge(maxT_ready, b + 1)
                q = q_h[k][:].bitcast(F32).rearrange("p h q -> p (h q)")
                m = maxT[:].bitcast(F32)
                full, rest = divmod(HALF, P)
                for dst, src in ((q[SIDE:SIDE + 1, 0:full * P], m[0:full, :]),
                                 (q[SIDE:SIDE + 1, full * P:HALF], m[full:full + 1, 0:rest]),
                                 (q[0:1, HALF:(full + 1) * P], m[full:full + 1, rest:P]),
                                 (q[0:1, (full + 1) * P:HQ], m[full + 1:MT, :])):
                    sp.dma_start(dst, src).then_inc(max_placed, 16)

            def store(b, k):
                sp.wait_ge(x1_ready, b + 1)
                sp.dma_start(x1_b[b], x1[k][:]).then_inc(x1_stored[k], 16)

            def load_x(b, k):
                sp.wait_ge(x_bo_ready, b - 1)
                sp.wait_ge(ln_done[0], b - 1)
                sp.dma_start(x_res[k][:], x[b]).then_inc(x_res_loaded[k], 16)

            def main(b, k, ahead, more):
                c, m = b + 1, 1 - k
                if more:
                    load_ctx(b + 3, m)
                if ahead >= 1:
                    copy_keys(c, m)
                if not is_first(b):
                    store(b - 1, m)
                if more:
                    load_x(b + 3, m)
                if ahead >= 1:
                    place_max(c, m)

            load_ctx(2, 0)
            copy_keys(0, 0)
            place_max(0, 0)
            load_x(2, 0)
            main(0, 0, 2, True)
            sp.dma_start(w1[:], W1.rearrange("e d h -> d e h")).then_inc(w_loaded, 16)
            sp.dma_start(w2[:], W2.rearrange("e (s p) d -> p (e s) d", p=P)).then_inc(w_loaded, 16)
            with sp.Fori(0, (B - 4) // 2) as i:
                main(2 * i + 1, 1, 2, True)
                main(2 * i + 2, 0, 2, True)
            for b in range(B - 3, B):
                main(b, b % 2, min(2, B - 1 - b), False)
            store(B - 1, 1)
            for k in range(2):
                sp.wait_ge(x1_stored[k], 16 * (B // 2))
            sp.dma_start(tok[:], x1_tok).then_inc(x1_loaded, 16)
            for n in range(4):
                sp.wait_ge(y_ready, n + 1)
                tiles = slice(4 * n, min(4 * n + 4, TT))
                sp.dma_start(out_tok[:, tiles], tok[:, tiles]).then_inc(out_stored, 16)
            sp.wait_ge(out_stored, 64)

        @block.gpsimd
        def _(pool):
            nc.gpsimd.memset(ident[:], 0.0).then_inc(blanks_ready, 1)
            for k in range(2):
                nc.gpsimd.memset(nat[k][:, :, KD:CR], 1.0).then_inc(ones_ready, 1)
            nc.gpsimd.memset(head_mask[:], 1.0).then_inc(blanks_ready, 1)
            nc.gpsimd.memset(side_mask[:], 1.0).then_inc(blanks_ready, 1)
            nc.gpsimd.memset(minus_half[:], -0.5).then_inc(blanks_ready, 1)
            nc.gpsimd.memset(ln_eps_c[:], LN_EPS).then_inc(blanks_ready, 1)
            nc.gpsimd.memset(lower[:], 1.0).then_inc(blanks_ready, 1)
            pick = sumT[0:2 * NE, 0:NE * P].rearrange("g (e p) -> g e p", e=NE)
            nc.gpsimd.memset(pick, 0.0).then_inc(blanks_ready, 1)
            pool.wait_ge(blanks_ready, 7)
            nc.gpsimd.affine_select(out=ident[:], in_=ident[:], compare_op=ALU.not_equal, fill=1.0,
                                    base=0, pattern=[[-1, P]], channel_multiplier=1).then_inc(consts_ready, 1)
            nc.gpsimd.affine_select(out=head_mask[:], in_=head_mask[:], compare_op=ALU.is_ge, fill=0.0,
                                    base=0, pattern=[[-HD, HEADS]], channel_multiplier=1).then_inc(consts_ready, 1)
            nc.gpsimd.affine_select(out=lower[:], in_=lower[:], compare_op=ALU.is_gt, fill=0.0,
                                    base=0, pattern=[[1, NE], [-1, NE]], channel_multiplier=0).then_inc(consts_ready, 1)
            nc.gpsimd.affine_select(out=pick, in_=pick, compare_op=ALU.not_equal, fill=1.0,
                                    base=0, pattern=[[-1, NE], [0, P]], channel_multiplier=1).then_inc(consts_ready, 1)
            pool.wait_ge(consts_ready, 4)
            nc.gpsimd.affine_select(out=head_mask[:], in_=head_mask[:], compare_op=ALU.is_ge, fill=0.0,
                                    base=HD - 1, pattern=[[HD, HEADS]], channel_multiplier=-1).then_inc(consts_ready, 1)
            nc.gpsimd.affine_select(out=pick, in_=pick, compare_op=ALU.not_equal, fill=1.0,
                                    base=-NE, pattern=[[-1, NE], [0, P]], channel_multiplier=1).then_inc(consts_ready, 1)
            pool.wait_ge(consts_ready, 6)
            nc.gpsimd.tensor_tensor(out=side_mask[:], in0=head_mask[:, 0:HEADS // 2], in1=head_mask[:, HEADS // 2:],
                                    op=ALU.add).then_inc(consts_ready, 1)
            pool.wait_ge(consts_ready, 7)

            def root(n, count):
                pool.wait_ge(ln_var[n], count)
                nc.gpsimd.tensor_tensor(out=var_eps[n][:], in0=mean_var[n][:, 1:2], in1=ln_eps_c[:], op=ALU.add
                                        ).then_inc(ln_eps[n], 1)
                pool.wait_ge(ln_eps[n], count)
                nc.gpsimd.tensor_tensor(out=rstd[n][:], in0=var_eps[n][:], in1=minus_half[:], op=ALU.pow
                                        ).then_inc(ln_rstd[n], 1)

            def diagonals(b, k):
                pool.wait_ge(q_copied, b + 1)
                for n in range(2):
                    heads8 = slice(n * HEADS // 2, (n + 1) * HEADS // 2)
                    nc.gpsimd.tensor_tensor(
                        out=q_h[k][:, heads8, :],
                        in0=q_full[:].rearrange("p (a q) -> p a q", a=1).to_broadcast([P, HEADS // 2, NQ]),
                        in1=head_mask[:, heads8].rearrange("p (h a) -> p h a", a=1).to_broadcast([P, HEADS // 2, NQ]),
                        op=ALU.mult).then_inc(q_h_ready, 1)
                pool.wait_ge(q_split, b + 1)
                for n in range(2):
                    last = nc.gpsimd.tensor_tensor(
                        out=q_lh[k][:, n],
                        in0=q_pair[:, n:n + 1, :].to_broadcast([P, HEADS // 2, NQ]),
                        in1=side_mask[:].rearrange("p (h a) -> p h a", a=1).to_broadcast([P, HEADS // 2, NQ]),
                        op=ALU.mult)
                last.then_inc(q_lh_ready, 1)

            def residual_bias(b, k, first):
                pool.wait_ge(x_res_loaded[k], uses(b, k))
                if not first:
                    pool.wait_ge(x1_ready, b - 1)
                    pool.wait_ge(x1_stored[k], uses(b, k) - 16)
                nc.gpsimd.tensor_tensor(out=x_bo[k][:], in0=x_res[k][:], in1=bo_gated[:],
                                        op=ALU.add).then_inc(x_bo_ready, 1)

            root(0, 1)
            diagonals(0, 0)
            root(0, 2)
            pool.wait_ge(q_lh_ready, 1)
            for n, rows in ((0, slice(SIDE, P)), (1, slice(0, SIDE))):
                for k in range(2):
                    nc.gpsimd.memset(key_h1[k][n][rows].bitcast(F32), 1.0).then_inc(ones_ready, 1)
                pool.wait_ge(ones_ready, 4 + 2 * n)
            for k in range(2):
                nc.gpsimd.memset(val[k][:, :, :, HD * 2:VW], 1.0).then_inc(ones_ready, 1)
            pool.wait_ge(ones_ready, 8)
            pool.wait_ge(bo_ready, 1)
            residual_bias(0, 0, True)

            def main(b, k, ahead):
                if ahead >= 1:
                    if not is_first(b):
                        pool.wait_ge(scored, KT * b)
                    diagonals(b + 1, 1 - k)
                if not is_first(b):
                    root(1, b)
                if ahead >= 1:
                    residual_bias(b + 1, 1 - k, is_first(b))
                if ahead >= 2:
                    root(0, b + 3)

            batches(pool, main)
            root(1, B)

            pool.wait_ge(scored, KT * B)
            pool.wait_ge(w_loaded, 32)
            for e in range(NE):
                nc.gpsimd.tensor_copy(w1_h[:, e], w1[:, e]).then_inc(w1_h_ready, 1)
                pool.wait_ge(w1_h_ready, e + 1)
                nc.gpsimd.tensor_tensor(out=w1_l[:, e], in0=w1[:, e], in1=w1_h[:, e].bitcast(F32),
                                        op=ALU.subtract).then_inc(w1_split, 1)

        @block.scalar
        def _(act):
            for dst, src in ((wq[:, 0, :], Wq), (bq_c[:, 0:1], column(bq)),
                             (wk_rows[0:KD, :], Wk), (wk_rows[KD:CR, :], row(bk)),
                             (wv_rows[0:KD, :], Wv), (wv_rows[KD:CR, :], row(bv))):
                act.dma_start(dst, src).then_inc(early_loaded, 16)

            def copy_ctx(b, g):
                act.wait_ge(ctx_transposed, NG * b + g + 1)
                nc.scalar.activation(ctxT[:, GT * g:GT * g + GT, :],
                                     prep_ps[0:CR, g % 2, 0:CK].rearrange("c (t p) -> c t p", p=KP),
                                     ACT.Copy).then_inc(ctx_copied, 1)

            def key_high(b, g):
                act.wait_ge(k_projected, NG * b + g + 1)
                if g == 0 and not is_first(b):
                    act.wait_ge(k_copied, 64 * b)
                src = prep_ps[:, 1 - g % 2, 0:CK].rearrange("c (t p) -> c t p", p=KP)
                tiles = slice(GT * g, GT * g + GT)
                nc.scalar.activation(key_h[:, tiles], src, ACT.Copy).then_inc(k_h_ready, 1)

            def copy_xnT(b):
                act.wait_ge(xn_transposed, b + 1)
                nc.scalar.activation(xnT[:], misc_ps[:, 0:NQ], ACT.Copy).then_inc(xnT_copied, 1)

            def copy_q(b):
                act.wait_ge(q_projected, b + 1)
                if not is_first(b):
                    act.wait_ge(q_lh_ready, b)
                nc.scalar.activation(q_pair[:], misc_ps[:, P + NQ:P + 2 * NQ].rearrange("p (a q) -> p a q", a=1)
                                     .to_broadcast([P, 2, NQ]), ACT.Identity, bias=bq_c[:, 1:2])
                nc.scalar.activation(q_full[:], misc_ps[:, P:P + NQ], ACT.Identity, bias=bq_c[:, 0:1]
                                     ).then_inc(q_copied, 1)

            def copy_max(b):
                act.wait_ge(max_transposed, b + 1)
                nc.scalar.activation(maxT[:], misc_ps[0:MT, P:2 * P], ACT.Copy).then_inc(maxT_ready, 1)

            def values(b, k, g):
                act.wait_ge(val_done, NG * b + g + 1)
                nc.scalar.activation(val[k][:, GT * g:GT * g + GT, :, 0:2 * HD],
                                     misc_ps[0:KP, :].rearrange("k (t p d) -> k t p d", t=GT, d=2 * HD),
                                     ACT.Copy).then_inc(val_copied, 1)

            def finish_acc(b):
                act.wait_ge(pv_done, KT * b + KT)
                nc.scalar.activation(acc[:].rearrange("p r a q -> p (r a q)"), pv_ps[:, 0:R * PQ],
                                     ACT.Copy).then_inc(acc_copied, 1)

            def finish_heads(b):
                act.wait_ge(heads_transposed, b + 1)
                nc.scalar.activation(headsT[:], misc_ps[:, 0:NQ], ACT.Copy).then_inc(headsT_copied, 1)

            def tokens_high(b):
                act.wait_ge(x2_transposed, b + 1)
                nc.scalar.activation(x2_h[:, bass.ds(b * NQ, NQ)], misc_ps[:, 0:NQ], ACT.Copy
                                     ).then_inc(x2_h_ready, 1)

            copy_ctx(0, 0)
            copy_ctx(0, 1)
            copy_xnT(0)
            act.wait_ge(wq_ready, 3)
            copy_q(0)
            copy_ctx(0, 2)
            for g in range(NG):
                key_high(0, g)
            for g in range(NG):
                values(0, 0, g)
            act.wait_ge(late_loaded, LATE_LOADS * 16)
            nc.scalar.activation(gate_tanh[:], gate_in[:], ACT.Tanh).then_inc(tanh_ready, 1)
            for g in range(NG):
                copy_ctx(1, g)
            act.wait_ge(b1_transposed, 1)
            nc.scalar.activation(b1_c[:], misc_ps[:, 0:NU], ACT.Copy).then_inc(xnT_copied, 1)
            key_high(1, 0)
            key_high(1, 1)
            copy_xnT(1)
            copy_max(0)
            copy_q(1)
            key_high(1, 2)

            def main(b, k, ahead):
                c, d, m, first = b + 1, b + 2, 1 - k, is_first(b)
                for t in range(KT):
                    act.wait_ge(scored, KT * b + t + 1)
                    if not (first and t < 2):
                        act.wait_ge(pv_done, KT * b + t - 1)
                    nc.scalar.activation(prob[t % 2][:].rearrange("p (n q) -> p n q", n=2),
                                         scores_ps[0:KP, t % 2, :, 0:HALF], ACT.Exp,
                                         scale=SCALE).then_inc(exp_done, 1)
                    if t == 0 and not first:
                        finish_acc(b - 1)
                    if t == 3 and not first:
                        finish_heads(b - 1)
                    if ahead >= 1 and t in VALUE_STEPS:
                        values(c, m, VALUE_STEPS.index(t))
                    if t == 7 and not first:
                        tokens_high(b - 1)
                    if ahead >= 2:
                        if t == 8:
                            copy_ctx(d, 0)
                            copy_ctx(d, 1)
                    if ahead >= 1 and t == 8:
                        copy_max(c)
                    if ahead >= 2 and t == 9:
                        copy_ctx(d, 2)
                    if ahead >= 2:
                        if t == 10:
                            key_high(d, 0)
                            key_high(d, 1)
                            copy_xnT(d)
                        if t == 11:
                            key_high(d, 2)
                            copy_q(d)

            batches(act, main)
            finish_acc(B - 1)
            finish_heads(B - 1)
            tokens_high(B - 1)
            act.wait_ge(gate_step, 3)
            nc.scalar.activation(lexp[:], logit[:], ACT.Exp).then_inc(gate_exp, 1)

            with act.Fori(0, CH) as n:
                for u in range(NU):
                    act.wait_ge(hidden_done, NU * n + u + 1)
                    if u >= 3:
                        act.wait_ge(gated_done, NU * n + u - 2)
                    nc.scalar.activation(gelu[:, u % 3, :], scores_ps[:, (u % 4) // 2, u % 2, 0:HALF], ACT.Gelu,
                                         bias=b1_c[:, u:u + 1]).then_inc(gelu_done, 1)
                act.wait_ge(summed, NU * n + NU)
                nc.scalar.activation(sumT[:, bass.ds(n * HALF, HALF)], pv_ps[:, 0:HALF],
                                     ACT.Copy).then_inc(sum_copied, 1)

        @block.vector
        def _(dve):
            H0, H1 = slice(0, SIDE), slice(SIDE, P)

            def norm_stats(n, src, b):
                nc.vector.bn_stats(stats[n][:], src).then_inc(ln_stats[n], 1)
                dve.wait_ge(ln_stats[n], b + 1)

            def norm_var(n):
                nc.vector.bn_aggr(mean_var[n][:], stats[n][:]).then_inc(ln_var[n], 1)

            def norm_apply(n, dst, src, b):
                dve.wait_ge(ln_rstd[n], b + 1)
                nc.vector.tensor_scalar(dst, src, mean_var[n][:, 0:1], rstd[n][:], ALU.subtract, ALU.mult
                                        ).then_inc(ln_done[n], 1)

            def key_low(b, g):
                dve.wait_ge(k_h_ready, NG * b + g + 1)
                tiles = slice(GT * g, GT * g + GT)
                nc.vector.tensor_tensor(key_l[:, tiles], prep_ps[:, 1 - g % 2, 0:CK].rearrange("c (t p) -> c t p", p=KP),
                                        key_h[:, tiles].bitcast(F32), ALU.subtract).then_inc(k_l_ready, 1)

            def split_q(b):
                dve.wait_ge(q_copied, b + 1)
                nc.vector.tensor_copy(q_round[:], q_full[:]).then_inc(q_rounded, 1)
                dve.wait_ge(q_rounded, b + 1)
                nc.vector.tensor_tensor(q_pair[H0, 0, :], q_full[H0], q_round[H0].bitcast(F32), ALU.subtract)
                nc.vector.tensor_tensor(q_pair[H1, 1, :], q_full[H1], q_round[H1].bitcast(F32), ALU.subtract
                                        ).then_inc(q_split, 1)

            def reduce_chunk(b, n):
                dve.wait_ge(max_scored, MN * b + n + 1)
                nc.vector.reduce_max(part_max[:, n // NG, n % NG:n % NG + 1], prep_ps[:, n % 2, 0:CK],
                                     AX_X).then_inc(max_reduced, 1)

            def negate_max(b):
                dve.wait_ge(max_reduced, MN * (b + 1))
                nc.vector.tensor_reduce(neg_max[:], part_max[:], AX_X, ALU.max, negate=True).then_inc(neg_max_ready, 1)

            def normalise(b):
                v = misc_ps[0:NQ, :].rearrange("q (r a j w) -> q r a j w", r=R, a=2, j=J)
                dve.wait_ge(acc_transposed, b + 1)
                nc.vector.reciprocal(den_inv[:].rearrange("q (n a) -> q n a", a=1),
                                     misc_ps[0:NQ, :].rearrange("q (n w) -> q n w", w=VW)[:, :, 2 * HD:2 * HD + 1]
                                     ).then_inc(den_ready, 1)
                dve.wait_ge(den_ready, b + 1)
                for a in range(2):
                    for r in range(R):
                        o = heads[:].rearrange("q (r j a d) -> q r a j d", r=R, j=J, a=2)[:, r, a]
                        d = den_inv[:].rearrange("q (r a j w) -> q r a j w", r=R, a=2, w=1)[:, r, a]
                        ins = nc.vector.tensor_tensor(o, v[:, r, a, :, HD * a:HD * a + HD],
                                                      d.to_broadcast([NQ, J, HD]), ALU.mult)
                ins.then_inc(heads_ready, 1)

            def residual(b, k):
                dve.wait_ge(projected, b + 1)
                dve.wait_ge(x_bo_ready, b + 1)
                nc.vector.scalar_tensor_tensor(out=x1[k][:], in0=misc_ps[0:NQ, 0:D], scalar=gate_tanh[0:NQ, 0:1],
                                               in1=x_bo[k][:], op0=ALU.mult, op1=ALU.add).then_inc(x1_ready, 1)
                dve.wait_ge(x1_ready, b + 1)
                norm_stats(1, x1[k][:], b)

            def tokens_low(b):
                dve.wait_ge(x2_h_ready, b + 1)
                cols = bass.ds(b * NQ, NQ)
                nc.vector.tensor_tensor(x2_l[:, cols], misc_ps[:, 0:NQ], x2_h[:, cols].bitcast(F32), ALU.subtract
                                        ).then_inc(x2_l_ready, 1)

            def load_stats(b, k):
                dve.wait_ge(x_res_loaded[k], uses(b, k))
                norm_stats(0, x_res[k][:], b)

            load_stats(0, 0)
            norm_var(0)
            norm_apply(0, xn[:], x_res[0][:], 0)
            dve.wait_ge(early_loaded, EARLY_LOADS * 16)
            nc.vector.tensor_copy(wq[:, 1, H0], wq[:, 0, H1]).then_inc(wq_ready, 1)
            nc.vector.tensor_copy(wq[:, 1, H1], wq[:, 0, H0]).then_inc(wq_ready, 1)
            nc.vector.tensor_copy(bq_c[H0, 1:2], bq_c[H1, 0:1])
            nc.vector.tensor_copy(bq_c[H1, 1:2], bq_c[H0, 0:1]).then_inc(wq_ready, 1)
            split_q(0)
            for g in range(NG):
                key_low(0, g)
            load_stats(1, 1)
            norm_var(0)
            for n in range(MN):
                dve.wait_ge(max_scored, n + 1)
                nc.vector.reduce_max(part_max[:, n // NG, n % NG:n % NG + 1], scores_ps[:, (n % 4) // 2, n % 2, 0:CK],
                                     AX_X).then_inc(max_reduced, 1)
                if n == 7:
                    norm_apply(0, xn[:], x_res[1][:], 1)
            negate_max(0)
            dve.wait_ge(tanh_ready, 1)
            nc.vector.tensor_scalar(bo_gated[:], bo_b[:], gate_tanh[0:NQ, 0:1], None, ALU.mult).then_inc(bo_ready, 1)
            key_low(1, 0)
            key_low(1, 1)
            key_low(1, 2)
            split_q(1)
            dve.wait_ge(late_loaded, LATE_LOADS * 16)
            nc.vector.tensor_copy(expert_pick[:], sumT[0:2 * NE, 0:NE * P].rearrange("g (e p) -> g e p", e=NE)
                                  ).then_inc(weights_split, 1)
            nc.vector.tensor_copy(wg_h[:], wg[:]).then_inc(weights_split, 1)
            nc.vector.tensor_copy(b2_h[:], b2_r[:]).then_inc(weights_split, 1)
            dve.wait_ge(weights_split, 3)
            nc.vector.tensor_tensor(wg_l[:], wg[:], wg_h[:].bitcast(F32), ALU.subtract).then_inc(weights_split, 1)
            nc.vector.tensor_tensor(b2_l[:], b2_r[:], b2_h[:].bitcast(F32), ALU.subtract).then_inc(weights_split, 1)

            def main(b, k, ahead):
                c, d, m, first = b + 1, b + 2, 1 - k, is_first(b)
                for t in range(KT):
                    if not first:
                        if t == 5:
                            residual(b - 1, m)
                            if ahead == 0:
                                norm_var(1)
                        if t == 6:
                            norm_apply(1, xn2[:], x1[m][:], b - 1)
                    for n in range(NG):
                        if t == 2 and n == 2 and not first:
                            normalise(b - 1)
                        if ahead >= 1 and 1 <= t <= 7:
                            if t == 7 and n == 1 and ahead >= 2:
                                load_stats(d, k)
                            reduce_chunk(c, NG * (t - 1) + n)
                            if t == 5 and n == 0 and not first:
                                norm_var(1)
                            if t == 7 and n == 1 and ahead >= 2:
                                norm_var(0)
                    if ahead >= 1 and t == 7:
                        negate_max(c)
                    if not first and t == 8:
                        tokens_low(b - 1)
                    if ahead >= 2:
                        if t == 8:
                            norm_apply(0, xn[:], x_res[k][:], d)
                        if t == 10:
                            key_low(d, 0)
                            key_low(d, 1)
                        if t == 11:
                            key_low(d, 2)
                            split_q(d)

            batches(dve, main)
            normalise(B - 1)
            residual(B - 1, 1)
            norm_var(1)
            norm_apply(1, xn2[:], x1[1][:], B - 1)
            tokens_low(B - 1)

            steps = [0]

            def step(ins):
                steps[0] += 1
                ins.then_inc(gate_step, 1)
                dve.wait_ge(gate_step, steps[0])

            def over_experts(v):
                return v.rearrange("p (t a) -> p t a", a=1).to_broadcast([P, TT, NE])

            dve.wait_ge(logits_done, 1)
            step(nc.vector.tensor_tensor(logit[:], misc_ps[:, 0:TT * NE].rearrange("p (t e) -> p t e", e=NE),
                                         bg_b[:].rearrange("p (a e) -> p a e", a=1).to_broadcast([P, TT, NE]),
                                         ALU.add))
            step(nc.vector.reduce_max(lmax[:], logit[:], AX_X))
            step(nc.vector.tensor_tensor(logit[:], logit[:], over_experts(lmax[:]), ALU.subtract))
            dve.wait_ge(gate_exp, 1)
            step(nc.vector.reduce_sum(lsum[:], lexp[:], AX_X))
            step(nc.vector.reciprocal(lmax[:], lsum[:]))
            step(nc.vector.tensor_tensor(gates[:], lexp[:], over_experts(lmax[:]), ALU.mult))
            other = gates[:].rearrange("p t (a f) -> p t a f", a=1).to_broadcast([P, TT, NE, NE])
            mine = gates[:].rearrange("p t (e a) -> p t e a", a=1).to_broadcast([P, TT, NE, NE])
            gt = cmp_gt.rearrange("p t (e f) -> p t e f", f=NE)
            eq = cmp_eq.rearrange("p t (e f) -> p t e f", f=NE)
            step(nc.vector.tensor_tensor(gt, other, mine, ALU.is_gt))
            step(nc.vector.tensor_tensor(eq, other, mine, ALU.is_equal))
            step(nc.vector.tensor_tensor(cmp_eq, cmp_eq,
                                         lower[:].rearrange("p e f -> p (e f)").rearrange("p (a n) -> p a n", a=1)
                                         .to_broadcast([P, TT, NE * NE]), ALU.mult))
            step(nc.vector.tensor_tensor(cmp_gt, cmp_gt, cmp_eq, ALU.add))
            step(nc.vector.reduce_sum(rank[:], gt, AX_X))
            step(nc.vector.tensor_scalar(rank[:], rank[:], TOP - 0.5, None, ALU.is_lt))
            step(nc.vector.tensor_tensor(gates[:], gates[:], rank[:], ALU.mult))
            step(nc.vector.reduce_sum(lsum[:], gates[:], AX_X))
            step(nc.vector.tensor_scalar(lsum[:], lsum[:], GATE_EPS, None, ALU.max))
            step(nc.vector.reciprocal(lmax[:], lsum[:]))
            step(nc.vector.tensor_tensor(gates[:], gates[:], over_experts(lmax[:]), ALU.mult))
            step(nc.vector.tensor_copy(gate_hl[:, :, 0:NE], gates[:]))
            step(nc.vector.tensor_tensor(gate_hl[:, :, NE:2 * NE], gates[:], gate_hl[:, :, 0:NE].bitcast(F32),
                                         ALU.subtract))
            for n in range(4):
                w = min(4, TT - 4 * n) * P
                dve.wait_ge(gates_transposed, n + 1)
                nc.vector.tensor_copy(gT2[:, 512 * n:512 * n + w], prep_ps[0:2 * NE, n % 2, 0:w]
                                      ).then_inc(gates_copied, 1)

            with dve.Fori(0, CH) as n:
                for u in range(NU):
                    dve.wait_ge(gelu_done, NU * n + u + 1)
                    if u % SL == 0:
                        dve.wait_ge(spread_done, NE * n + u // SL + 1)
                    if u >= 3:
                        dve.wait_ge(summed, NU * n + u - 2)
                    nc.vector.tensor_tensor(gated[:, u % 3, :], prep_ps[:, (u // SL) % 2, 0:HALF], gelu[:, u % 3, :],
                                            ALU.mult).then_inc(gated_done, 1)
            dve.wait_ge(x1_loaded, 16)
            for n in range(4):
                dve.wait_ge(y_transposed, n + 1)
                w = min(4, TT - 4 * n)
                tiles = tok[:, 4 * n:4 * n + w, :].rearrange("p t d -> p (t d)")
                nc.vector.scalar_tensor_tensor(out=tiles, in0=scores_ps[:, n // 2, n % 2, 0:w * P],
                                               scalar=gate_tanh[:, 1:2], in1=tiles,
                                               op0=ALU.mult, op1=ALU.add).then_inc(y_ready, 1)

        @block.tensor
        def _(pe):
            mm = nc.tensor.matmul

            def ctx_transpose(b, k, g):
                if g == 0:
                    pe.wait_ge(nat_loaded[k], uses(b, k))
                    if not (isinstance(b, int) and b < 2):
                        pe.wait_ge(max_reduced, MN * b)
                if g == 2:
                    pe.wait_ge(ctx_copied, NG * b + 1)
                for t in range(GT):
                    last = nc.tensor.transpose(prep_ps[0:CR, g % 2, t * KP:(t + 1) * KP],
                                               nat[k][:, GT * g + t, :], ident[0:KP, 0:KP])
                last.then_inc(ctx_transposed, 1)

            def transpose_xn(b):
                nc.tensor.transpose(misc_ps[:, 0:NQ], xn[:], ident[0:NQ, 0:NQ]).then_inc(xn_transposed, 1)

            def project_q(b):
                pe.wait_ge(xnT_copied, 1 if is_first(b) else b + 2)
                for n in range(2):
                    last = mm(misc_ps[:, P + n * NQ:P + (n + 1) * NQ], wq[:, n, :], xnT[:], start=True, stop=True)
                last.then_inc(q_projected, 1)

            def project_keys(b, g):
                if g == 0:
                    pe.wait_ge(ctx_copied, NG * b + 2)
                elif g == 1:
                    pe.wait_ge(ctx_copied, NG * b + 3)
                else:
                    pe.wait_ge(k_l_ready, NG * b + 1)
                mm(prep_ps[:, 1 - g % 2, 0:CK], wk_rows[:], ctxT[:, GT * g:GT * g + GT, :],
                   start=True, stop=True).then_inc(k_projected, 1)

            def make_values(b, g):
                if g == 0:
                    pe.wait_ge(q_copied, b + 1)
                elif g == 1:
                    if not (isinstance(b, int) and b < 2):
                        pe.wait_ge(x1_ready, b - 1)
                    pe.wait_ge(val_copied, NG * b + g)
                else:
                    pe.wait_ge(val_copied, NG * b + g)
                for t in range(GT):
                    last = mm(misc_ps[0:KP, t * D:(t + 1) * D], ctxT[:, GT * g + t, :], wv_rows[:],
                              start=True, stop=True)
                last.then_inc(val_done, 1)

            def max_chunk(b, k, n):
                if n == HALF // P * NG:
                    pe.wait_ge(q_h_ready, 2 * b + 2)
                if n == 0:
                    pe.wait_ge(q_h_ready, 2 * b + 1)
                    pe.wait_ge(k_l_ready, NG * b + 2)
                elif n == 1:
                    pe.wait_ge(k_l_ready, NG * b + 3)
                else:
                    pe.wait_ge(max_reduced, MN * b + n - 1)
                g = n % NG
                mm(prep_ps[:, n % 2, 0:CK], q_h[k][:].rearrange("p h q -> p (h q)")[:, n // NG * P:(n // NG + 1) * P],
                   key_h[:, GT * g:GT * g + GT, :], start=True, stop=True).then_inc(max_scored, 1)

            def ready_for_max(b, first):
                pe.wait_ge(neg_max_ready, b + 2)
                if first:
                    pe.wait_ge(val_copied, 2 * NG)
                else:
                    pe.wait_ge(x2_l_ready, b)

            def max_row(b):
                nc.tensor.transpose(misc_ps[0:MT, P:2 * P], neg_max[:], ident[:]).then_inc(max_transposed, 1)

            def score_half(b, k, t, n, first):
                if t == 0 and n == 0:
                    pe.wait_ge(k_copied, 64 * b + 64)
                    pe.wait_ge(q_lh_ready, b + 1)
                    pe.wait_ge(max_placed, 64 * b + 64)
                if n == 0 and not (first and t < 2):
                    pe.wait_ge(exp_done, KT * b + t - 1)
                o = scores_ps[0:KP, t % 2, n, 0:HALF]
                mm(o, key_hl[k][n][:, t, :], q_lh[k][:, n].rearrange("p h q -> p (h q)"), start=True, stop=False)
                last = mm(o, key_h1[k][n][:, t, :],
                          q_h[k][:].rearrange("p h q -> p (h q)")[:, n * HALF:(n + 1) * HALF],
                          start=False, stop=True)
                if n == 1:
                    last.then_inc(scored, 1)

            def value_tile(b, k, t, first):
                pe.wait_ge(exp_done, KT * b + t + 1)
                if t == 0:
                    pe.wait_ge(val_copied, NG * b + NG)
                    if not first:
                        pe.wait_ge(acc_copied, b)
                for r in range(R):
                    for j in range(J):
                        p = J * r + j
                        last = mm(pv_ps[VW * j:VW * j + VW, r * PQ:(r + 1) * PQ], val[k][:, t, p, :],
                                  prob[t % 2][:, p * PQ:(p + 1) * PQ], start=(t == 0 and r == 0), stop=(t == KT - 1),
                                  skip_group_check=True)
                last.then_inc(pv_done, 1)

            def transpose_acc(b):
                for r in range(R):
                    for a in range(2):
                        n = 2 * r + a
                        last = nc.tensor.transpose(misc_ps[0:NQ, n * P:(n + 1) * P], acc[:, r, a, :], ident[:])
                last.then_inc(acc_transposed, 1)

            def transpose_heads(b):
                nc.tensor.transpose(misc_ps[:, 0:NQ], heads[:], ident[0:NQ, 0:NQ]).then_inc(heads_transposed, 1)

            def project(b):
                pe.wait_ge(headsT_copied, b + 1)
                mm(misc_ps[0:NQ, 0:D], headsT[:], wo[:], start=True, stop=True).then_inc(projected, 1)

            def transpose_x2(b):
                nc.tensor.transpose(misc_ps[:, 0:NQ], xn2[:], ident[0:NQ, 0:NQ]).then_inc(x2_transposed, 1)

            pe.wait_ge(consts_ready, 1)
            pe.wait_ge(ones_ready, 2)
            ctx_transpose(0, 0, 0)
            ctx_transpose(0, 0, 1)
            pe.wait_ge(ln_done[0], 1)
            transpose_xn(0)
            pe.wait_ge(wq_ready, 3)
            project_q(0)
            ctx_transpose(0, 0, 2)
            for g in range(NG):
                project_keys(0, g)
            make_values(0, 0)
            for n in range(MN):
                if n == 0:
                    pe.wait_ge(q_h_ready, 2)
                    pe.wait_ge(k_h_ready, NG)
                if n >= 4:
                    pe.wait_ge(max_reduced, n - 3)
                g = n % NG
                mm(scores_ps[:, (n % 4) // 2, n % 2, 0:CK],
                   q_h[0][:].rearrange("p h q -> p (h q)")[:, n // NG * P:(n // NG + 1) * P],
                   key_h[:, GT * g:GT * g + GT, :], start=True, stop=True).then_inc(max_scored, 1)
                if n in (4, 6):
                    make_values(0, n // 2 - 1)
                if n == 8:
                    pe.wait_ge(k_l_ready, NG)
                    for g in range(NG):
                        ctx_transpose(1, 1, g)
                if n == 10:
                    pe.wait_ge(late_loaded, LATE_LOADS * 16)
                    pe.wait_ge(val_copied, NG)
                    nc.tensor.transpose(misc_ps[:, 0:NU], b1_rows[:], ident[0:NU, 0:NU]).then_inc(b1_transposed, 1)
            project_keys(1, 0)
            pe.wait_ge(xnT_copied, 2)
            pe.wait_ge(ln_done[0], 2)
            project_keys(1, 1)
            transpose_xn(1)
            pe.wait_ge(xnT_copied, 3)
            pe.wait_ge(neg_max_ready, 1)
            max_row(0)
            pe.wait_ge(maxT_ready, 1)
            project_q(1)
            project_keys(1, 2)
            pe.wait_ge(ones_ready, 8)

            def main(b, k, ahead):
                c, d, m, first = b + 1, b + 2, 1 - k, is_first(b)
                for t in range(KT):
                    maxima = ahead >= 1 and 1 <= t <= 7
                    if t == 0 and not first:
                        value_tile(b - 1, m, KT - 1, False)
                    score_half(b, k, t, 0, first)
                    if maxima:
                        max_chunk(c, m, NG * (t - 1))
                    score_half(b, k, t, 1, first)
                    if maxima:
                        max_chunk(c, m, NG * (t - 1) + 1)
                    if ahead >= 2 and t == 10:
                        project_keys(d, 0)
                    if not first:
                        if t == 2:
                            pe.wait_ge(acc_copied, b)
                            if ahead >= 1:
                                pe.wait_ge(val_copied, NG * c + 1)
                            else:
                                pe.wait_ge(x2_l_ready, b - 1)
                        if t == 3:
                            pe.wait_ge(heads_ready, b)
                        if t == 7:
                            pe.wait_ge(ln_done[1], b)
                            if ahead >= 1:
                                pe.wait_ge(val_copied, NG * c + NG)
                    if ahead == 1 and t == 8:
                        ready_for_max(b, first)
                    if ahead >= 2 and t == 10:
                        pe.wait_ge(ln_done[0], d + 1)
                        pe.wait_ge(maxT_ready, c + 1)
                    if t >= 1:
                        value_tile(b, k, t - 1, first)
                    if not first:
                        if t == 2:
                            transpose_acc(b - 1)
                        if t == 3:
                            transpose_heads(b - 1)
                        if t == 4:
                            project(b - 1)
                        if t == 7:
                            transpose_x2(b - 1)
                    if ahead >= 1 and t in VALUE_STEPS:
                        make_values(c, VALUE_STEPS.index(t))
                    if maxima:
                        max_chunk(c, m, NG * (t - 1) + 2)
                    if ahead >= 2:
                        if t == 8:
                            ctx_transpose(d, k, 0)
                            ready_for_max(b, first)
                            ctx_transpose(d, k, 1)
                        if t == 9:
                            ctx_transpose(d, k, 2)
                        if t == 10:
                            transpose_xn(d)
                            project_keys(d, 1)
                        if t == 11:
                            project_q(d)
                            project_keys(d, 2)
                    if ahead >= 1 and t == 8:
                        max_row(c)

            batches(pe, main)
            value_tile(B - 1, 1, KT - 1, False)
            pe.wait_ge(acc_copied, B)
            pe.wait_ge(x2_l_ready, B - 1)
            transpose_acc(B - 1)
            pe.wait_ge(heads_ready, B)
            transpose_heads(B - 1)
            project(B - 1)
            pe.wait_ge(ln_done[1], B)
            transpose_x2(B - 1)

            pe.wait_ge(x2_l_ready, B)
            pe.wait_ge(weights_split, 5)
            for t in range(TT):
                o = misc_ps[:, t * NE:(t + 1) * NE]
                mm(o, x2_h[:, t * P:(t + 1) * P], wg_h[:], start=True, stop=False)
                mm(o, x2_h[:, t * P:(t + 1) * P], wg_l[:], start=False, stop=False)
                last = mm(o, x2_l[:, t * P:(t + 1) * P], wg_h[:], start=False, stop=True)
            last.then_inc(logits_done, 1)
            pe.wait_ge(gate_step, GATE_STEPS)
            for n in range(4):
                if n >= 2:
                    pe.wait_ge(gates_copied, n - 1)
                w = min(4, TT - 4 * n)
                for t in range(4 * n, 4 * n + w):
                    last = nc.tensor.transpose(prep_ps[0:2 * NE, n % 2, (t % 4) * P:(t % 4 + 1) * P],
                                               gate_hl[:, t, :].bitcast(F32), ident[:])
                last.then_inc(gates_transposed, 1)
            pe.wait_ge(gates_copied, 4)
            pe.wait_ge(w1_split, NE)
            pe.wait_ge(w_loaded, 32)

            with pe.Fori(0, CH) as n:
                tokens = bass.ds(n * HALF, HALF)

                def hidden(u):
                    e, s = u // SL, u % SL
                    o = scores_ps[:, (u % 4) // 2, u % 2, 0:HALF]
                    wh = w1_h[:, e, s * P:(s + 1) * P]
                    mm(o, wh, x2_h[:, tokens], start=True, stop=False)
                    mm(o, wh, x2_l[:, tokens], start=False, stop=False)
                    mm(o, w1_l[:, e, s * P:(s + 1) * P], x2_h[:, tokens], start=False, stop=True
                       ).then_inc(hidden_done, 1)

                def accumulate(u):
                    mm(pv_ps[:, 0:HALF], w2[:, u, :], gated[:, u % 3, :], start=False, stop=(u == NU - 1)
                       ).then_inc(summed, 1)

                for u in range(NU):
                    if u >= 4:
                        pe.wait_ge(gelu_done, NU * n + u - 3)
                    if u % SL == 0 and u >= 2 * SL:
                        pe.wait_ge(gated_done, NU * n + u - SL)
                    if u == 2:
                        pe.wait_ge(gelu_done, NU * n + 1)
                    hidden(u)
                    if u % SL == 0:
                        e = u // SL
                        mm(prep_ps[:, e % 2, 0:HALF], expert_pick[:, e, :], gT2[:, tokens],
                           start=True, stop=True).then_inc(spread_done, 1)
                    if u == 2:
                        mm(pv_ps[:, 0:HALF], b2_h[:], gT2[:, tokens], start=True, stop=False)
                        mm(pv_ps[:, 0:HALF], b2_l[:], gT2[:, tokens], start=False, stop=False)
                    if u >= 2:
                        pe.wait_ge(gated_done, NU * n + u - 1)
                        accumulate(u - 2)
                for u in (NU - 2, NU - 1):
                    pe.wait_ge(gated_done, NU * n + u + 1)
                    accumulate(u)

            for n in range(4):
                pe.wait_ge(sum_copied, min(4, (4 * n + 4) * P // HALF + 1))
                w = min(4, TT - 4 * n)
                for t in range(4 * n, 4 * n + w):
                    last = nc.tensor.transpose(scores_ps[:, n // 2, n % 2, (t % 4) * P:(t % 4 + 1) * P],
                                               sumT[:, t * P:(t + 1) * P], ident[:])
                last.then_inc(y_transposed, 1)


_INS = ['x', 'ctx_768', 'g_xattn', 'g_ffn', 'L0_xattn_Wq', 'L0_xattn_bq', 'L0_xattn_Wk', 'L0_xattn_bk',
        'L0_xattn_Wv', 'L0_xattn_bv', 'L0_xattn_Wo', 'L0_xattn_bo', 'L0_ffn_Wg', 'L0_ffn_bg', 'L0_ffn_W1',
        'L0_ffn_b1', 'L0_ffn_W2', 'L0_ffn_b2']
_OUT = ((32, 56, 128), 'float32')


def kernel(**inputs):
    import numpy as _np
    import concourse.bacc as _bacc
    from concourse import mybir as _mybir
    from concourse.bass_utils import run_bass_kernel_spmd as _run

    nc = _bacc.Bacc("TRN2", target_bir_lowering=False, num_devices=1)
    arrays, args = {}, []
    for name in _INS:
        a = _np.ascontiguousarray(inputs[name])
        arrays[f"in_{name}_dram"] = a
        args.append(nc.dram_tensor(f"in_{name}_dram", a.shape, _mybir.dt.from_np(a.dtype), kind="ExternalInput").ap())
    shape, dtype = _OUT
    out = nc.dram_tensor("out_0_dram", shape, _mybir.dt.from_np(_np.dtype(dtype)), kind="ExternalOutput").ap()
    gated_xattn_moe(nc, *args, out)
    r = _run(nc, [arrays], core_ids=[0])
    return r.results[0]["out_0_dram"]
```

```python
from contextlib import ExitStack

import concourse.bass as bass
from concourse import mybir

F32 = mybir.dt.float32
F32R = mybir.dt.float32r
ALU = mybir.AluOpType
ACT = mybir.ActivationFunctionType
AX_X = mybir.AxisListType.X

P = 128


def gated_xattn_moe(nc, x, ctx, g_xattn, g_ffn, Wq, bq, Wk, bk, Wv, bv, Wo, bo,
                    Wg, bg, W1, b1, W2, b2, out):
    B, NQ, D = x.shape
    _, NK, KD = ctx.shape
    HEADS = 16
    HD = D // HEADS
    SCALE = float(HD) ** -0.5
    LN_EPS, GATE_EPS = 1e-5, 1e-12
    KT = 12
    KP = NK // KT
    HQ = HEADS * NQ
    HALF = HQ // 2
    QUADS = 4
    QH = HEADS // QUADS
    QR = QH * HD
    QN = QH * NQ
    SR = 3 * QR + 1
    CR = KD + 1
    GT = 4
    NG = KT // GT
    CK = GT * KP
    MT = HQ // P
    MN = MT * NG
    PAIRS = HEADS // 2
    PQ = 2 * NQ
    VW = 32
    J, R = 4, 2
    TOK = B * NQ
    TT = TOK // P
    NE, HID = W1.shape[0], W1.shape[2]
    SL = HID // P
    NU = NE * SL
    CH = TOK // HALF
    TOP = 2
    VALUE_STEPS = (0, 5, 6)
    MAX_STEPS = (2, 3, 3, 2, 3, 3, 3, 2, 0, 0, 0, 0)
    GATE_STEPS = 19
    GATED = TT // 2
    SLOTS = 4
    LAG = 3
    STAGES = 3
    EARLY_LOADS, LATE_LOADS = 6, 8
    assert KT * KP == NK and MT * P == HQ and TT * P == TOK and CH * HALF == TOK and D == P

    with ExitStack() as stack:
        def sb(name, shape, dt=F32):
            return stack.enter_context(nc.sbuf_tensor(name, shape, dt))

        def psum(name, shape):
            return stack.enter_context(nc.psum_tensor(name, shape, F32))

        def sem(name):
            return stack.enter_context(nc.semaphore(name))

        x1_dram = nc.dram_tensor("x1_scratch", [TOK, D], F32, kind="Internal").ap()

        scores_ps = psum("scores_ps", [P, 2, 2, 512])
        prep_ps = psum("prep_ps", [P, 2, 512])
        pv_ps = psum("pv_ps", [P, 512])
        misc_ps = psum("misc_ps", [P, 512])

        ident = sb("ident", [P, P])
        head_mask = sb("head_mask", [P, HEADS])
        pair_mask = sb("pair_mask", [P, HEADS // 2])
        quad_mask = sb("quad_mask", [P, QH])
        minus_half = sb("minus_half", [NQ, 1])
        ln_eps_c = sb("ln_eps_c", [NQ, 1])
        wq = sb("wq", [P, D])
        wq3 = sb("wq3", [P, QUADS, 3, QR])
        bq_c = sb("bq_c", [P, 1])
        bq3 = sb("bq3", [3 * QR, QUADS])
        wk_rows = sb("wk_rows", [CR, D])
        wv_rows = sb("wv_rows", [CR, D])
        wo = sb("wo", [P, D])
        gate_in = sb("gate_in", [P, 2])
        gate_tanh = sb("gate_tanh", [P, 2])
        bo_b = sb("bo_b", [NQ, D])
        bo_gated = sb("bo_gated", [NQ, D])
        wg = sb("wg", [P, NE])
        wg_h = sb("wg_h", [P, NE], F32R)
        wg_l = sb("wg_l", [P, NE], F32R)
        bg_b = sb("bg_b", [P, NE])
        w1_h = sb("w1_h", [P, NE, HID], F32R)
        w1_l = sb("w1_l", [P, NE, HID], F32R)
        b_rows = sb("b_rows", [NU + NE, P])
        b_cols = sb("b_cols", [P, NU + NE])
        lower = sb("lower", [P, NE, NE])
        expert_pick = sb("expert_pick", [2 * NE, NE, P], F32R)

        nat = [sb(f"nat{k}", [KP, KT, CR]) for k in range(2)]
        ctxT = sb("ctxT", [CR, KT, KP])
        key_h = sb("key_h", [P, KT, KP], F32R)
        key_l = sb("key_l", [P, KT, KP], F32R)
        maxT = sb("maxT", [MT, P], F32R)
        keys = sb("keys", [P, 2, QUADS, KT, KP], F32R)
        q_quad = [sb(f"q_quad{k}", [P, QUADS, QN], F32R) for k in range(2)]
        q_h = sb("q_h", [P, HEADS, NQ], F32R)
        q_full = sb("q_full", [P, NQ])
        q_mix = sb("q_mix", [3 * QR, QUADS, NQ])
        q_round = sb("q_round", [3 * QR, QUADS, NQ], F32R)
        val_all = sb("val_all", [P, 2, KT, PAIRS, VW])
        val = [val_all[0:KP, k] for k in range(2)]
        prob = [sb(f"prob{k}", [KP, HQ]) for k in range(2)]
        x_res = [sb(f"x_res{k}", [NQ, D]) for k in range(2)]
        x_bo = [sb(f"x_bo{k}", [NQ, D]) for k in range(2)]
        x1 = [sb(f"x1_{k}", [NQ, D]) for k in range(2)]
        xn = sb("xn", [NQ, D])
        xnT = sb("xnT", [P, NQ])
        stats = [sb(f"stats{n}", [NQ, 6]) for n in range(2)]
        mean_var = [sb(f"mean_var{n}", [NQ, 2]) for n in range(2)]
        var_eps = [sb(f"var_eps{n}", [NQ, 1]) for n in range(2)]
        rstd = [sb(f"rstd{n}", [NQ, 1]) for n in range(2)]
        xn2 = sb("xn2", [NQ, D])
        part_max = sb("part_max", [P, MT, NG])
        neg_max = sb("neg_max", [P, MT])
        acc = sb("acc", [P, R, 2, NQ])
        den_inv = sb("den_inv", [NQ, HEADS])
        heads = sb("heads", [NQ, D])
        headsT = sb("headsT", [P, NQ])

        x2_h = sb("x2_h", [P, TOK], F32R)
        x2_l = sb("x2_l", [P, TOK], F32R)
        keys_flat = keys[:].rearrange("p a g t n -> p (a g t n)")
        w2_hl = keys_flat[:, 0:2 * NU * D].rearrange("p (e a s d) -> p e a s d", e=NE, a=2, s=SL)
        w2_early = QUADS * NK // (2 * HID)
        gelu_hl = keys_flat[:, 2 * NU * D:2 * NU * D + 2 * SLOTS * HALF]
        gelu_h, gelu_l = (gelu_hl[:, n * SLOTS * HALF:(n + 1) * SLOTS * HALF].rearrange("p (s q) -> p s q", s=SLOTS)
                          for n in range(2))
        val0_flat = val_all[:, 0].rearrange("p t a d -> p (t a d)")
        gelu = val0_flat[:, 0:SLOTS * HALF].rearrange("p (s q) -> p s q", s=SLOTS)
        scaled_out = val0_flat[:, SLOTS * HALF:(SLOTS + 2) * HALF].rearrange("p (s q) -> p s q", s=2)
        gate_rows = val_all[:, 1].rearrange("p t a d -> p (t a d)")[:, 0:2 * HALF].rearrange("p (s q) -> p s q", s=2)
        gate_hl = sb("gate_hl", [P, TT, 2 * NE], F32R)
        tok = sb("tok", [P, TT, D])
        stage = tok[:].rearrange("p t d -> p (t d)")[:, 0:STAGES * HID].rearrange("p (n h) -> p n h", n=STAGES)
        sumT = sb("sumT", [P, TOK])
        gT2 = sb("gT2", [2 * NE, TOK], F32R)
        logit = sb("logit", [P, TT, NE])
        lmax = sb("lmax", [P, TT])
        lexp = sb("lexp", [P, TT, NE])
        lsum = sb("lsum", [P, TT])
        gates = sb("gates", [P, TT, NE])
        rank = sb("rank", [P, TT, NE])
        cmp_gt = sumT[:, HALF * 2:HALF * 3].rearrange("p (t n) -> p t n", t=GATED)
        cmp_eq = sumT[:, HALF * 3:].rearrange("p (t n) -> p t n", t=GATED)

        early_loaded = sem("early_loaded")
        late_loaded = sem("late_loaded")
        stage_loaded = [sem(f"stage_loaded{n}") for n in range(STAGES)]
        nat_loaded = [sem(f"nat_loaded{k}") for k in range(2)]
        x_res_loaded = [sem(f"x_res_loaded{k}") for k in range(2)]
        x1_stored = [sem(f"x1_stored{k}") for k in range(2)]
        x1_loaded = sem("x1_loaded")
        out_stored = sem("out_stored")
        blanks_ready = sem("blanks_ready")
        consts_ready = sem("consts_ready")
        ones_ready = sem("ones_ready")
        tanh_ready = sem("tanh_ready")
        weights_split = sem("weights_split")
        wq_ready = sem("wq_ready")
        bo_ready = sem("bo_ready")
        b_transposed = sem("b_transposed")
        ln_stats = [sem(f"ln{n}_stats") for n in (1, 2)]
        ln_var = [sem(f"ln{n}_var") for n in (1, 2)]
        ln_eps = [sem(f"ln{n}_eps") for n in (1, 2)]
        ln_rstd = [sem(f"ln{n}_rstd") for n in (1, 2)]
        ln_done = [sem(f"ln{n}_done") for n in (1, 2)]
        xn_transposed = sem("xn_transposed")
        xnT_copied = sem("xnT_copied")
        q_projected = sem("q_projected")
        q_copied = sem("q_copied")
        q_rounded = sem("q_rounded")
        q_split = sem("q_split")
        q_h_ready = sem("q_h_ready")
        q_quad_ready = sem("q_quad_ready")
        ctx_transposed = sem("ctx_transposed")
        ctx_copied = sem("ctx_copied")
        k_projected = sem("k_projected")
        k_h_ready = sem("k_h_ready")
        k_l_ready = sem("k_l_ready")
        k_copied = sem("k_copied")
        max_scored = sem("max_scored")
        max_reduced = sem("max_reduced")
        neg_max_ready = sem("neg_max_ready")
        max_transposed = sem("max_transposed")
        maxT_ready = sem("maxT_ready")
        max_placed = sem("max_placed")
        val_done = sem("val_done")
        val_copied = sem("val_copied")
        scored = sem("scored")
        exp_done = sem("exp_done")
        pv_done = sem("pv_done")
        acc_copied = sem("acc_copied")
        acc_transposed = sem("acc_transposed")
        den_ready = sem("den_ready")
        heads_ready = sem("heads_ready")
        heads_transposed = sem("heads_transposed")
        headsT_copied = sem("headsT_copied")
        projected = sem("projected")
        x_bo_ready = sem("x_bo_ready")
        x1_ready = sem("x1_ready")
        x2_transposed = sem("x2_transposed")
        x2_h_ready = sem("x2_h_ready")
        x2_l_ready = sem("x2_l_ready")
        w_h_ready = sem("w_h_ready")
        w_split = sem("w_split")
        logits_done = sem("logits_done")
        gate_step = sem("gate_step")
        gate_exp = sem("gate_exp")
        gates_transposed = sem("gates_transposed")
        gates_copied = sem("gates_copied")
        hidden_done = sem("hidden_done")
        gelu_done = sem("gelu_done")
        gelu_h_ready = sem("gelu_h_ready")
        gelu_l_ready = sem("gelu_l_ready")
        spread_done = sem("spread_done")
        spread_copied = sem("spread_copied")
        multiplied = sem("multiplied")
        scaled = sem("scaled")
        summed = sem("summed")
        y_transposed = sem("y_transposed")
        y_ready = sem("y_ready")

        ctx_v = ctx.rearrange("b (p t) c -> b p t c", t=KT)
        x1_b = x1_dram.rearrange("(b q) d -> b q d", q=NQ)
        x1_tok = x1_dram.rearrange("(t p) d -> p t d", p=P)
        out_tok = out.rearrange("b q d -> (b q) d").rearrange("(t p) d -> p t d", p=P)

        def row(v):
            return v.rearrange("(a n) -> a n", a=1)

        def column(v):
            return v.rearrange("(p a) -> p a", a=1)

        def batches(engine, main):
            main(0, 0, 2)
            with engine.Fori(0, (B - 4) // 2) as i:
                main(2 * i + 1, 1, 2)
                main(2 * i + 2, 0, 2)
            for b in range(B - 3, B):
                main(b, b % 2, min(2, B - 1 - b))

        def is_first(b):
            return isinstance(b, int) and b == 0

        def uses(b, k):
            return 16 * (b // 2) + 16 if isinstance(b, int) else 8 * (b - k) + 16

        def result_ps(n, e):
            bank = pv_ps if e % 2 == 0 or (isinstance(n, int) and n == 0 and e == 1) else misc_ps
            return bank[:, 0:HALF]

        block = stack.enter_context(nc.Block())

        @block.sync
        def _(sp):
            sp.dma_start(x_res[0][:], x[0]).then_inc(x_res_loaded[0], 16)
            sp.dma_start(nat[0][:, :, 0:KD], ctx_v[0]).then_inc(nat_loaded[0], 16)
            sp.wait_ge(early_loaded, EARLY_LOADS * 16)
            sp.wait_ge(nat_loaded[0], 16)
            sp.dma_start(x_res[1][:], x[1]).then_inc(x_res_loaded[1], 16)
            sp.dma_start(nat[1][:, :, 0:KD], ctx_v[1]).then_inc(nat_loaded[1], 16)
            for dst, src in ((gate_in[:, 0:1], row(g_xattn).to_broadcast([P, 1])),
                             (gate_in[:, 1:2], row(g_ffn).to_broadcast([P, 1])),
                             (bo_b[:], row(bo).to_broadcast([NQ, D])),
                             (wo[:], Wo), (wg[:], Wg), (bg_b[:], row(bg).to_broadcast([P, NE])),
                             (b_rows[0:NU, :], b1.rearrange("e (s p) -> (e s) p", p=P)), (b_rows[NU:, :], b2)):
                sp.dma_start(dst, src).then_inc(late_loaded, 16)

            def load_ctx(b, k):
                sp.wait_ge(ctx_transposed, NG * b - NG)
                sp.dma_start(nat[k][:, :, 0:KD], ctx_v[b]).then_inc(nat_loaded[k], 16)

            def copy_keys(b, k):
                sp.wait_ge(k_l_ready, NG * b + NG)
                if not (isinstance(b, int) and b < 2):
                    sp.wait_ge(scored, KT * b - KT)
                for g in range(QUADS):
                    group = slice(g * QR, (g + 1) * QR)
                    for n, part in enumerate((key_h, key_l, key_h)):
                        sp.dma_start(keys[n * QR:(n + 1) * QR, k, g].bitcast(F32), part[group].bitcast(F32)
                                     ).then_inc(k_copied, 16)

            def place_max(b, k):
                sp.wait_ge(maxT_ready, b + 1)
                sp.dma_start(q_quad[k][SR - 1:SR].bitcast(F32).rearrange("a g n -> a (g n)"), maxT[:].bitcast(F32)
                             ).then_inc(max_placed, 16)

            def store(b, k):
                sp.wait_ge(x1_ready, b + 1)
                sp.dma_start(x1_b[b], x1[k][:]).then_inc(x1_stored[k], 16)

            def load_x(b, k):
                sp.wait_ge(x_bo_ready, b - 1)
                sp.wait_ge(ln_done[0], b - 1)
                sp.dma_start(x_res[k][:], x[b]).then_inc(x_res_loaded[k], 16)

            def main(b, k, ahead, more):
                c, m = b + 1, 1 - k
                if more:
                    load_ctx(b + 3, m)
                if ahead >= 1:
                    copy_keys(c, m)
                if not is_first(b):
                    store(b - 1, m)
                if more:
                    load_x(b + 3, m)
                if ahead >= 1:
                    place_max(c, m)

            def load_weights(i):
                if i >= STAGES:
                    sp.wait_ge(w_split, i - STAGES + 1)
                src = W1[i:i + 1].rearrange("e d (s h) -> d (e s) h", s=SL) if i < NE else \
                    W2[i - NE:i - NE + 1].rearrange("e (s p) d -> p (e s) d", p=P)
                sp.dma_start(stage[:, i % STAGES].rearrange("p (s h) -> p s h", s=SL), src
                             ).then_inc(stage_loaded[i % STAGES], 16)

            load_ctx(2, 0)
            copy_keys(0, 0)
            place_max(0, 0)
            load_x(2, 0)
            main(0, 0, 2, True)
            for i in range(STAGES):
                load_weights(i)
            with sp.Fori(0, (B - 4) // 2) as i:
                main(2 * i + 1, 1, 2, True)
                main(2 * i + 2, 0, 2, True)
            main(B - 3, 1, 2, False)
            for i in range(3, 6):
                load_weights(i)
            main(B - 2, 0, 1, False)
            for i in range(6, 9):
                load_weights(i)
            main(B - 1, 1, 0, False)
            for i in range(9, 14):
                load_weights(i)
            store(B - 1, 1)
            for i in range(14, 2 * NE):
                load_weights(i)
            sp.wait_ge(w_split, 2 * NE)
            for k in range(2):
                sp.wait_ge(x1_stored[k], 16 * (B // 2))
            sp.dma_start(tok[:], x1_tok).then_inc(x1_loaded, 16)
            for n in range(4):
                sp.wait_ge(y_ready, n + 1)
                tiles = slice(4 * n, min(4 * n + 4, TT))
                sp.dma_start(out_tok[:, tiles], tok[:, tiles]).then_inc(out_stored, 16)
            sp.wait_ge(out_stored, 64)

        @block.gpsimd
        def _(pool):
            nc.gpsimd.memset(ident[:], 0.0).then_inc(blanks_ready, 1)
            for k in range(2):
                nc.gpsimd.memset(nat[k][:, :, KD:CR], 1.0).then_inc(ones_ready, 1)
            nc.gpsimd.memset(head_mask[:], 1.0).then_inc(blanks_ready, 1)
            nc.gpsimd.memset(minus_half[:], -0.5).then_inc(blanks_ready, 1)
            nc.gpsimd.memset(ln_eps_c[:], LN_EPS).then_inc(blanks_ready, 1)
            nc.gpsimd.memset(lower[:], 1.0).then_inc(blanks_ready, 1)
            pick = sumT[0:2 * NE, 0:NE * P].rearrange("g (e p) -> g e p", e=NE)
            nc.gpsimd.memset(pick, 0.0).then_inc(blanks_ready, 1)
            pool.wait_ge(blanks_ready, 6)
            nc.gpsimd.affine_select(out=ident[:], in_=ident[:], compare_op=ALU.not_equal, fill=1.0,
                                    base=0, pattern=[[-1, P]], channel_multiplier=1).then_inc(consts_ready, 1)
            nc.gpsimd.affine_select(out=head_mask[:], in_=head_mask[:], compare_op=ALU.is_ge, fill=0.0,
                                    base=0, pattern=[[-HD, HEADS]], channel_multiplier=1).then_inc(consts_ready, 1)
            nc.gpsimd.affine_select(out=lower[:], in_=lower[:], compare_op=ALU.is_gt, fill=0.0,
                                    base=0, pattern=[[1, NE], [-1, NE]], channel_multiplier=0).then_inc(consts_ready, 1)
            nc.gpsimd.affine_select(out=pick, in_=pick, compare_op=ALU.not_equal, fill=1.0,
                                    base=0, pattern=[[-1, NE], [0, P]], channel_multiplier=1).then_inc(consts_ready, 1)
            pool.wait_ge(consts_ready, 4)
            nc.gpsimd.affine_select(out=head_mask[:], in_=head_mask[:], compare_op=ALU.is_ge, fill=0.0,
                                    base=HD - 1, pattern=[[HD, HEADS]], channel_multiplier=-1).then_inc(consts_ready, 1)
            nc.gpsimd.affine_select(out=pick, in_=pick, compare_op=ALU.not_equal, fill=1.0,
                                    base=-NE, pattern=[[-1, NE], [0, P]], channel_multiplier=1).then_inc(consts_ready, 1)
            pool.wait_ge(consts_ready, 6)
            nc.gpsimd.tensor_tensor(out=pair_mask[:], in0=head_mask[:, 0:HEADS // 2], in1=head_mask[:, HEADS // 2:],
                                    op=ALU.add).then_inc(consts_ready, 1)
            pool.wait_ge(consts_ready, 7)
            nc.gpsimd.tensor_tensor(out=quad_mask[:], in0=pair_mask[:, 0:QH], in1=pair_mask[:, QH:],
                                    op=ALU.add).then_inc(consts_ready, 1)
            pool.wait_ge(consts_ready, 8)

            def root(n, count):
                pool.wait_ge(ln_var[n], count)
                nc.gpsimd.tensor_tensor(out=var_eps[n][:], in0=mean_var[n][:, 1:2], in1=ln_eps_c[:], op=ALU.add
                                        ).then_inc(ln_eps[n], 1)
                pool.wait_ge(ln_eps[n], count)
                nc.gpsimd.tensor_tensor(out=rstd[n][:], in0=var_eps[n][:], in1=minus_half[:], op=ALU.pow
                                        ).then_inc(ln_rstd[n], 1)

            def diagonals(b, k):
                pool.wait_ge(q_copied, b + 1)
                for n in range(2):
                    heads8 = slice(n * HEADS // 2, (n + 1) * HEADS // 2)
                    nc.gpsimd.tensor_tensor(
                        out=q_h[:, heads8, :],
                        in0=q_full[:].rearrange("p (a q) -> p a q", a=1).to_broadcast([P, HEADS // 2, NQ]),
                        in1=head_mask[:, heads8].rearrange("p (h a) -> p h a", a=1).to_broadcast([P, HEADS // 2, NQ]),
                        op=ALU.mult).then_inc(q_h_ready, 1)
                pool.wait_ge(q_split, b + 1)
                if not (isinstance(b, int) and b < 2):
                    pool.wait_ge(scored, KT * b - KT)
                for g in range(QUADS):
                    last = nc.gpsimd.tensor_tensor(
                        out=q_quad[k][0:3 * QR, g].rearrange("p (h q) -> p h q", q=NQ),
                        in0=q_mix[:, g:g + 1, :].to_broadcast([3 * QR, QH, NQ]),
                        in1=quad_mask[0:3 * QR].rearrange("p (h a) -> p h a", a=1).to_broadcast([3 * QR, QH, NQ]),
                        op=ALU.mult)
                last.then_inc(q_quad_ready, 1)

            def residual_bias(b, k, first):
                pool.wait_ge(x_res_loaded[k], uses(b, k))
                if not first:
                    pool.wait_ge(x1_ready, b - 1)
                    pool.wait_ge(x1_stored[k], uses(b, k) - 16)
                nc.gpsimd.tensor_tensor(out=x_bo[k][:], in0=x_res[k][:], in1=bo_gated[:],
                                        op=ALU.add).then_inc(x_bo_ready, 1)

            root(0, 1)
            diagonals(0, 0)
            root(0, 2)
            pool.wait_ge(q_quad_ready, 1)
            pool.wait_ge(ln_rstd[0], 2)
            for k in range(2):
                nc.gpsimd.memset(keys[SR - 1:SR, k].bitcast(F32), 1.0).then_inc(ones_ready, 1)
            pool.wait_ge(ones_ready, 4)
            for k in range(2):
                nc.gpsimd.memset(val[k][:, :, :, HD * 2:VW], 1.0).then_inc(ones_ready, 1)
            pool.wait_ge(ones_ready, 6)
            pool.wait_ge(bo_ready, 1)
            residual_bias(0, 0, True)

            def split_weights(i):
                n = i % STAGES
                high, low = (w1_h[:, i], w1_l[:, i]) if i < NE else \
                    (w2_hl[:, i - NE, a].rearrange("p s d -> p (s d)") for a in range(2))
                pool.wait_ge(stage_loaded[n], 16 * (i // STAGES + 1))
                nc.gpsimd.tensor_copy(high, stage[:, n]).then_inc(w_h_ready, 1)
                pool.wait_ge(w_h_ready, i + 1)
                nc.gpsimd.tensor_tensor(out=low, in0=stage[:, n], in1=high.bitcast(F32),
                                        op=ALU.subtract).then_inc(w_split, 1)

            def main(b, k, ahead):
                if ahead >= 1:
                    diagonals(b + 1, 1 - k)
                if isinstance(b, int) and b >= B - 3:
                    for e in (0, 1, 2) if b == B - 3 else (3, 4, 5) if b == B - 2 else (6, 7):
                        split_weights(e)
                if not is_first(b):
                    root(1, b)
                if ahead >= 1:
                    residual_bias(b + 1, 1 - k, is_first(b))
                if ahead >= 2:
                    root(0, b + 3)

            batches(pool, main)
            pool.wait_ge(scored, KT * (B - 1))
            for e in range(4):
                split_weights(NE + e)
            root(1, B)
            for e in range(4, NE):
                if e == w2_early:
                    pool.wait_ge(scored, KT * B)
                split_weights(NE + e)

        @block.scalar
        def _(act):
            for dst, src in ((wq[:], Wq), (bq_c[:], column(bq)),
                             (wk_rows[0:KD, :], Wk), (wk_rows[KD:CR, :], row(bk)),
                             (wv_rows[0:KD, :], Wv), (wv_rows[KD:CR, :], row(bv))):
                act.dma_start(dst, src).then_inc(early_loaded, 16)

            def copy_ctx(b, g):
                act.wait_ge(ctx_transposed, NG * b + g + 1)
                nc.scalar.activation(ctxT[:, GT * g:GT * g + GT, :],
                                     prep_ps[0:CR, g % 2, 0:CK].rearrange("c (t p) -> c t p", p=KP),
                                     ACT.Copy).then_inc(ctx_copied, 1)

            def key_high(b, g):
                act.wait_ge(k_projected, NG * b + g + 1)
                if g == 0 and not is_first(b):
                    act.wait_ge(k_copied, 16 * 3 * QUADS * b)
                src = prep_ps[:, 1 - g % 2, 0:CK].rearrange("c (t p) -> c t p", p=KP)
                tiles = slice(GT * g, GT * g + GT)
                nc.scalar.activation(key_h[:, tiles], src, ACT.Copy).then_inc(k_h_ready, 1)

            def copy_xnT(b):
                act.wait_ge(xn_transposed, b + 1)
                nc.scalar.activation(xnT[:], misc_ps[:, 0:NQ], ACT.Copy).then_inc(xnT_copied, 1)

            def copy_max(b):
                act.wait_ge(max_transposed, b + 1)
                nc.scalar.activation(maxT[:], misc_ps[0:MT, P:2 * P], ACT.Copy).then_inc(maxT_ready, 1)

            def values(b, k, g):
                act.wait_ge(val_done, NG * b + g + 1)
                nc.scalar.activation(val[k][:, GT * g:GT * g + GT, :, 0:2 * HD],
                                     misc_ps[0:KP, :].rearrange("k (t p d) -> k t p d", t=GT, d=2 * HD),
                                     ACT.Copy).then_inc(val_copied, 1)

            def finish_acc(b):
                act.wait_ge(pv_done, KT * b + KT)
                nc.scalar.activation(acc[:].rearrange("p r a q -> p (r a q)"), pv_ps[:, 0:R * PQ],
                                     ACT.Copy).then_inc(acc_copied, 1)

            def finish_heads(b):
                act.wait_ge(heads_transposed, b + 1)
                nc.scalar.activation(headsT[:], misc_ps[:, 0:NQ], ACT.Copy).then_inc(headsT_copied, 1)

            def tokens_high(b):
                act.wait_ge(x2_transposed, b + 1)
                nc.scalar.activation(x2_h[:, bass.ds(b * NQ, NQ)], misc_ps[:, 0:NQ], ACT.Copy
                                     ).then_inc(x2_h_ready, 1)

            copy_ctx(0, 0)
            copy_ctx(0, 1)
            copy_xnT(0)
            copy_ctx(0, 2)
            for g in range(NG):
                key_high(0, g)
            for g in range(NG):
                values(0, 0, g)
            act.wait_ge(late_loaded, LATE_LOADS * 16)
            nc.scalar.activation(gate_tanh[:], gate_in[:], ACT.Tanh).then_inc(tanh_ready, 1)
            for g in range(NG):
                copy_ctx(1, g)
            act.wait_ge(b_transposed, 1)
            nc.scalar.activation(b_cols[:], misc_ps[:, 0:NU + NE], ACT.Copy).then_inc(xnT_copied, 1)
            key_high(1, 0)
            key_high(1, 1)
            copy_xnT(1)
            copy_max(0)
            key_high(1, 2)

            def main(b, k, ahead):
                c, d, m, first = b + 1, b + 2, 1 - k, is_first(b)
                for t in range(KT):
                    act.wait_ge(scored, KT * b + t + 1)
                    if not (first and t < 2):
                        act.wait_ge(pv_done, KT * b + t - 1)
                    nc.scalar.activation(prob[t % 2][:].rearrange("p (n q) -> p n q", n=2),
                                         scores_ps[0:KP, t % 2, :, 0:HALF], ACT.Exp,
                                         scale=SCALE).then_inc(exp_done, 1)
                    if t == 0 and not first:
                        finish_acc(b - 1)
                    if t == 3 and not first:
                        finish_heads(b - 1)
                    if ahead >= 1 and t in VALUE_STEPS:
                        values(c, m, VALUE_STEPS.index(t))
                    if t == 7 and not first:
                        tokens_high(b - 1)
                    if ahead >= 2:
                        if t == 8:
                            copy_ctx(d, 0)
                            copy_ctx(d, 1)
                    if ahead >= 1 and t == 8:
                        copy_max(c)
                    if ahead >= 2 and t == 9:
                        copy_ctx(d, 2)
                        copy_xnT(d)
                    if ahead >= 2:
                        if t == 10:
                            key_high(d, 0)
                            key_high(d, 1)
                        if t == 11:
                            key_high(d, 2)

                if ahead == 1:
                    gate_exps(0)

            def gate_exps(part):
                act.wait_ge(gate_step, GATE_STEPS * part + 3)
                tiles = slice(GATED * part, GATED * part + GATED)
                nc.scalar.activation(lexp[:, tiles], logit[:, tiles], ACT.Exp).then_inc(gate_exp, 1)

            batches(act, main)

            def gelu_high(n, u):
                act.wait_ge(gelu_done, NU * n + u + 1)
                if not (isinstance(n, int) and NU * n + u < SLOTS):
                    act.wait_ge(multiplied, NU * n + u + 1 - SLOTS)
                nc.scalar.activation(gelu_h[:, u % SLOTS, :], gelu[:, u % SLOTS, :], ACT.Copy
                                     ).then_inc(gelu_h_ready, 1)

            def chunk(n):
                begin = isinstance(n, int)
                if begin:
                    finish_acc(B - 1)
                for u in range(NU):
                    act.wait_ge(hidden_done, NU * n + u + 1)
                    if not (begin and u < SLOTS):
                        act.wait_ge(gelu_l_ready, NU * n + u + 1 - SLOTS)
                    nc.scalar.activation(gelu[:, u % SLOTS, :], scores_ps[:, (u % 4) // 2, u % 2, 0:HALF], ACT.Gelu,
                                         bias=b_cols[:, u:u + 1]).then_inc(gelu_done, 1)
                    if not (begin and u == 0):
                        gelu_high(n, u - 1)
                    if begin and u == 3:
                        finish_heads(B - 1)
                    if begin and u == 6:
                        tokens_high(B - 1)
                    if begin and u == 11:
                        gate_exps(1)

            chunk(0)
            with act.Fori(1, CH) as n:
                chunk(n)
            gelu_high(CH - 1, NU - 1)

        @block.vector
        def _(dve):

            def norm_stats(n, src, b):
                nc.vector.bn_stats(stats[n][:], src).then_inc(ln_stats[n], 1)
                dve.wait_ge(ln_stats[n], b + 1)

            def norm_var(n):
                nc.vector.bn_aggr(mean_var[n][:], stats[n][:]).then_inc(ln_var[n], 1)

            def norm_apply(n, dst, src, b):
                dve.wait_ge(ln_rstd[n], b + 1)
                nc.vector.tensor_scalar(dst, src, mean_var[n][:, 0:1], rstd[n][:], ALU.subtract, ALU.mult
                                        ).then_inc(ln_done[n], 1)

            def key_low(b, g):
                dve.wait_ge(k_h_ready, NG * b + g + 1)
                tiles = slice(GT * g, GT * g + GT)
                nc.vector.tensor_tensor(key_l[:, tiles],
                                        prep_ps[:, 1 - g % 2, 0:CK].rearrange("c (t p) -> c t p", p=KP),
                                        key_h[:, tiles].bitcast(F32), ALU.subtract).then_inc(k_l_ready, 1)

            def copy_q(b):
                dve.wait_ge(q_projected, b + 1)
                if not is_first(b):
                    dve.wait_ge(q_quad_ready, b)
                nc.vector.tensor_tensor(q_mix[:], misc_ps[0:3 * QR, 2 * P:2 * P + QUADS * NQ]
                                        .rearrange("p (g q) -> p g q", q=NQ),
                                        bq3[:].rearrange("p (g a) -> p g a", a=1).to_broadcast([3 * QR, QUADS, NQ]),
                                        ALU.add)
                nc.vector.tensor_scalar(q_full[:], misc_ps[:, P:P + NQ], bq_c[:], None, ALU.add).then_inc(q_copied, 1)

            def split_q(b):
                low = slice(2 * QR, 3 * QR)
                dve.wait_ge(q_copied, b + 1)
                nc.vector.tensor_copy(q_round[low], q_mix[low]).then_inc(q_rounded, 1)
                dve.wait_ge(q_rounded, b + 1)
                nc.vector.tensor_tensor(q_mix[low], q_mix[low], q_round[low].bitcast(F32), ALU.subtract
                                        ).then_inc(q_split, 1)

            def reduce_chunk(b, n):
                dve.wait_ge(max_scored, MN * b + n + 1)
                nc.vector.reduce_max(part_max[:, n // NG, n % NG:n % NG + 1], prep_ps[:, n % 2, 0:CK],
                                     AX_X).then_inc(max_reduced, 1)

            def negate_max(b):
                dve.wait_ge(max_reduced, MN * (b + 1))
                nc.vector.tensor_reduce(neg_max[:], part_max[:], AX_X, ALU.max, negate=True).then_inc(neg_max_ready, 1)

            def denominators(b):
                dve.wait_ge(acc_transposed, b + 1)
                nc.vector.reciprocal(den_inv[:].rearrange("q (n a) -> q n a", a=1),
                                     misc_ps[0:NQ, :].rearrange("q (n w) -> q n w", w=VW)[:, :, 2 * HD:2 * HD + 1]
                                     ).then_inc(den_ready, 1)

            def normalise(b):
                v = misc_ps[0:NQ, :].rearrange("q (r a j w) -> q r a j w", r=R, a=2, j=J)
                dve.wait_ge(den_ready, b + 1)
                for a in range(2):
                    ins = nc.vector.tensor_tensor(
                        heads[:].rearrange("q (r j a d) -> q r a j d", r=R, j=J, a=2)[:, :, a],
                        v[:, :, a, :, HD * a:HD * a + HD],
                        den_inv[:].rearrange("q (r a j w) -> q r a j w", r=R, a=2, w=1)[:, :, a]
                        .to_broadcast([NQ, R, J, HD]), ALU.mult)
                ins.then_inc(heads_ready, 1)

            def residual(b, k):
                dve.wait_ge(projected, b + 1)
                dve.wait_ge(x_bo_ready, b + 1)
                nc.vector.scalar_tensor_tensor(out=x1[k][:], in0=misc_ps[0:NQ, 0:D], scalar=gate_tanh[0:NQ, 0:1],
                                               in1=x_bo[k][:], op0=ALU.mult, op1=ALU.add).then_inc(x1_ready, 1)

            def x1_stats(b, k):
                dve.wait_ge(x1_ready, b + 1)
                norm_stats(1, x1[k][:], b)

            def tokens_low(b):
                dve.wait_ge(x2_h_ready, b + 1)
                cols = bass.ds(b * NQ, NQ)
                nc.vector.tensor_tensor(x2_l[:, cols], misc_ps[:, 0:NQ], x2_h[:, cols].bitcast(F32), ALU.subtract
                                        ).then_inc(x2_l_ready, 1)

            def load_stats(b, k):
                dve.wait_ge(x_res_loaded[k], uses(b, k))
                norm_stats(0, x_res[k][:], b)

            load_stats(0, 0)
            norm_var(0)
            norm_apply(0, xn[:], x_res[0][:], 0)
            dve.wait_ge(early_loaded, EARLY_LOADS * 16)
            nc.vector.tensor_copy(wq3[:], wq[:].rearrange("p (g a i) -> p g a i", a=1, i=QR)
                                  .to_broadcast([P, QUADS, 3, QR]))
            for g in range(QUADS):
                for n in range(3):
                    last = nc.vector.tensor_copy(bq3[n * QR:(n + 1) * QR, g:g + 1], bq_c[g * QR:(g + 1) * QR])
            last.then_inc(wq_ready, 1)
            copy_q(0)
            split_q(0)
            for g in range(NG):
                key_low(0, g)
            load_stats(1, 1)
            norm_var(0)
            for n in range(MN):
                dve.wait_ge(max_scored, n + 1)
                nc.vector.reduce_max(part_max[:, n // NG, n % NG:n % NG + 1], scores_ps[:, (n % 4) // 2, n % 2, 0:CK],
                                     AX_X).then_inc(max_reduced, 1)
                if n == 7:
                    norm_apply(0, xn[:], x_res[1][:], 1)
            negate_max(0)
            dve.wait_ge(tanh_ready, 1)
            nc.vector.tensor_scalar(bo_gated[:], bo_b[:], gate_tanh[0:NQ, 0:1], None, ALU.mult).then_inc(bo_ready, 1)
            key_low(1, 0)
            key_low(1, 1)
            copy_q(1)
            split_q(1)
            key_low(1, 2)
            dve.wait_ge(late_loaded, LATE_LOADS * 16)
            nc.vector.tensor_copy(expert_pick[:], sumT[0:2 * NE, 0:NE * P].rearrange("g (e p) -> g e p", e=NE)
                                  ).then_inc(weights_split, 1)
            nc.vector.tensor_copy(wg_h[:], wg[:]).then_inc(weights_split, 1)
            dve.wait_ge(weights_split, 2)
            nc.vector.tensor_tensor(wg_l[:], wg[:], wg_h[:].bitcast(F32), ALU.subtract).then_inc(weights_split, 1)

            def main(b, k, ahead):
                c, d, m, first = b + 1, b + 2, 1 - k, is_first(b)
                for t in range(KT):
                    if not first:
                        if t == 5:
                            residual(b - 1, m)
                            if ahead == 0:
                                x1_stats(b - 1, m)
                                norm_var(1)
                        if t == 6:
                            norm_apply(1, xn2[:], x1[m][:], b - 1)
                    if ahead == 0 and t == 4:
                        for n in range(2):
                            copy_gates(0, n, prep_ps[:, n])
                    for n in range(NG):
                        if t == 2 and n == 2 and not first:
                            denominators(b - 1)
                        if ahead >= 1 and n < MAX_STEPS[t]:
                            if t == 7 and n == 1 and ahead >= 2:
                                load_stats(d, k)
                            reduce_chunk(c, sum(MAX_STEPS[:t]) + n)
                            if t == 5 and n == 0 and not first:
                                x1_stats(b - 1, m)
                            if t == 5 and n == 1 and not first:
                                norm_var(1)
                            if t == 7 and n == 1 and ahead >= 2:
                                norm_var(0)
                    if t == 2 and not first:
                        normalise(b - 1)
                    if ahead >= 1 and t == 7:
                        negate_max(c)
                    if not first and t == 8:
                        tokens_low(b - 1)
                    if ahead >= 2:
                        if t == 8:
                            norm_apply(0, xn[:], x_res[k][:], d)
                        if t == 10:
                            key_low(d, 0)
                            copy_q(d)
                            split_q(d)
                            key_low(d, 1)
                        if t == 11:
                            key_low(d, 2)

                if ahead == 1:
                    for i in range(GATE_STEPS):
                        gate(0, i)

            def gate(part, i):
                if i == 0:
                    dve.wait_ge(logits_done, part + 1)
                else:
                    dve.wait_ge(gate_step, GATE_STEPS * part + i)
                t = slice(GATED * part, GATED * part + GATED)
                lo, ex, ga, ra, ma, su = (v[:, t] for v in (logit, lexp, gates, rank, lmax, lsum))

                def over_experts(v):
                    return v.rearrange("p (t a) -> p t a", a=1).to_broadcast([P, GATED, NE])

                if i == 0:
                    ins = nc.vector.tensor_tensor(
                        lo, misc_ps[:, 0:GATED * NE].rearrange("p (t e) -> p t e", e=NE),
                        bg_b[:].rearrange("p (a e) -> p a e", a=1).to_broadcast([P, GATED, NE]), ALU.add)
                elif i == 1:
                    ins = nc.vector.reduce_max(ma, lo, AX_X)
                elif i == 2:
                    ins = nc.vector.tensor_tensor(lo, lo, over_experts(ma), ALU.subtract)
                elif i == 3:
                    dve.wait_ge(gate_exp, part + 1)
                    ins = nc.vector.reduce_sum(su, ex, AX_X)
                elif i == 4:
                    ins = nc.vector.reciprocal(ma, su)
                elif i == 5:
                    ins = nc.vector.tensor_tensor(ga, ex, over_experts(ma), ALU.mult)
                elif i in (6, 7):
                    other = ga.rearrange("p t (a f) -> p t a f", a=1).to_broadcast([P, GATED, NE, NE])
                    mine = ga.rearrange("p t (e a) -> p t e a", a=1).to_broadcast([P, GATED, NE, NE])
                    ins = nc.vector.tensor_tensor(
                        (cmp_gt if i == 6 else cmp_eq).rearrange("p t (e f) -> p t e f", f=NE),
                        other, mine, ALU.is_gt if i == 6 else ALU.is_equal)
                elif i == 8:
                    ins = nc.vector.tensor_tensor(
                        cmp_eq, cmp_eq, lower[:].rearrange("p e f -> p (e f)").rearrange("p (a n) -> p a n", a=1)
                        .to_broadcast([P, GATED, NE * NE]), ALU.mult)
                elif i == 9:
                    ins = nc.vector.tensor_tensor(cmp_gt, cmp_gt, cmp_eq, ALU.add)
                elif i == 10:
                    ins = nc.vector.reduce_sum(ra, cmp_gt.rearrange("p t (e f) -> p t e f", f=NE), AX_X)
                elif i == 11:
                    ins = nc.vector.tensor_scalar(ra, ra, TOP - 0.5, None, ALU.is_lt)
                elif i == 12:
                    ins = nc.vector.tensor_tensor(ga, ga, ra, ALU.mult)
                elif i == 13:
                    ins = nc.vector.reduce_sum(su, ga, AX_X)
                elif i == 14:
                    ins = nc.vector.tensor_scalar(su, su, GATE_EPS, None, ALU.max)
                elif i == 15:
                    ins = nc.vector.reciprocal(ma, su)
                elif i == 16:
                    ins = nc.vector.tensor_tensor(ga, ga, over_experts(ma), ALU.mult)
                elif i == 17:
                    ins = nc.vector.tensor_copy(gate_hl[:, t, 0:NE], ga)
                else:
                    ins = nc.vector.tensor_tensor(gate_hl[:, t, NE:2 * NE], ga, gate_hl[:, t, 0:NE].bitcast(F32),
                                                  ALU.subtract)
                ins.then_inc(gate_step, 1)

            def copy_gates(part, n, bank):
                first, w = (GATED * part + 4 * n) * P, (4, GATED - 4)[n] * P
                dve.wait_ge(gates_transposed, 2 * part + n + 1)
                nc.vector.tensor_copy(gT2[:, first:first + w], bank[0:2 * NE, 0:w]).then_inc(gates_copied, 1)

            batches(dve, main)

            def gelu_low(n, u):
                dve.wait_ge(gelu_h_ready, NU * n + u + 1)
                nc.vector.tensor_tensor(gelu_l[:, u % SLOTS, :], gelu[:, u % SLOTS, :],
                                        gelu_h[:, u % SLOTS, :].bitcast(F32), ALU.subtract).then_inc(gelu_l_ready, 1)

            def scale(n, e):
                dve.wait_ge(multiplied, SL * (NE * n + e + 1))
                dve.wait_ge(spread_copied, NE * n + e + 1)
                if not (isinstance(n, int) and NE * n + e < 2):
                    dve.wait_ge(summed, NE * n + e - 1)
                nc.vector.scalar_tensor_tensor(out=scaled_out[:, e % 2, :], in0=result_ps(n, e),
                                               scalar=b_cols[:, NU + e % NE:NU + e % NE + 1],
                                               in1=gate_rows[:, e % 2, :], op0=ALU.add, op1=ALU.mult).then_inc(scaled, 1)

            def add(n, e, cols):
                dve.wait_ge(scaled, NE * n + e + 1)
                if e == 0:
                    ins = nc.vector.tensor_copy(sumT[:, cols], scaled_out[:, 0, :])
                else:
                    ins = nc.vector.tensor_tensor(sumT[:, cols], sumT[:, cols], scaled_out[:, e % 2, :], ALU.add)
                ins.then_inc(summed, 1)

            def copy_spread(n, e):
                dve.wait_ge(spread_done, NE * n + e + 1)
                nc.vector.tensor_copy(gate_rows[:, e % 2, :], prep_ps[:, e % 2, 0:HALF]).then_inc(spread_copied, 1)

            def chunk(n):
                begin = isinstance(n, int)
                tokens = bass.ds(n * HALF, HALF)
                for u in range(NU):
                    if begin and u == 0:
                        denominators(B - 1)
                        normalise(B - 1)
                    if begin and u == 3:
                        residual(B - 1, 1)
                        x1_stats(B - 1, 1)
                        norm_var(1)
                    if begin and u == 4:
                        norm_apply(1, xn2[:], x1[1][:], B - 1)
                    if begin and u in (NU - 3, NU - 2):
                        copy_gates(1, u - (NU - 3), prep_ps[:, 0])
                    gelu_low(n, u)
                    if begin and u == 5:
                        tokens_low(B - 1)
                    e = (u - SL - 1) // SL if u % SL == 1 else (u - SL - 2) // SL
                    cols = tokens if e >= 0 else bass.ds(n * HALF - HALF, HALF)
                    if u % SL == 1 and not (begin and e < 0):
                        scale(n, e)
                    if u % SL == 2 and not (begin and e < 0):
                        add(n, e, cols)
                    if u % SL == 3:
                        copy_spread(n, u // SL)
                    if begin and 7 <= u < 7 + GATE_STEPS:
                        gate(1, u - 7)

            chunk(0)
            with dve.Fori(1, CH) as n:
                chunk(n)
            scale(CH, -1)
            add(CH, -1, slice(TOK - HALF, TOK))
            dve.wait_ge(x1_loaded, 16)
            for n in range(4):
                dve.wait_ge(y_transposed, n + 1)
                w = min(4, TT - 4 * n)
                tiles = tok[:, 4 * n:4 * n + w, :].rearrange("p t d -> p (t d)")
                nc.vector.scalar_tensor_tensor(out=tiles, in0=scores_ps[:, n // 2, n % 2, 0:w * P],
                                               scalar=gate_tanh[:, 1:2], in1=tiles,
                                               op0=ALU.mult, op1=ALU.add).then_inc(y_ready, 1)

        @block.tensor
        def _(pe):
            mm = nc.tensor.matmul

            def ctx_transpose(b, k, g):
                if g == 0:
                    pe.wait_ge(nat_loaded[k], uses(b, k))
                    if not (isinstance(b, int) and b < 2):
                        pe.wait_ge(max_reduced, MN * b)
                if g == 2:
                    pe.wait_ge(ctx_copied, NG * b + 1)
                for t in range(GT):
                    last = nc.tensor.transpose(prep_ps[0:CR, g % 2, t * KP:(t + 1) * KP],
                                               nat[k][:, GT * g + t, :], ident[0:KP, 0:KP])
                last.then_inc(ctx_transposed, 1)

            def transpose_xn(b):
                nc.tensor.transpose(misc_ps[:, 0:NQ], xn[:], ident[0:NQ, 0:NQ]).then_inc(xn_transposed, 1)

            def project_q(b):
                pe.wait_ge(xnT_copied, 1 if is_first(b) else b + 2)
                mm(misc_ps[:, P:P + NQ], wq[:], xnT[:], start=True, stop=True)
                for g in range(QUADS):
                    last = mm(misc_ps[0:3 * QR, 2 * P + g * NQ:2 * P + (g + 1) * NQ],
                              wq3[:, g].rearrange("p a i -> p (a i)"), xnT[:], start=True, stop=True)
                last.then_inc(q_projected, 1)

            def project_keys(b, g):
                if g == 0:
                    pe.wait_ge(ctx_copied, NG * b + 2)
                elif g == 1:
                    pe.wait_ge(ctx_copied, NG * b + 3)
                else:
                    pe.wait_ge(k_l_ready, NG * b + 1)
                mm(prep_ps[:, 1 - g % 2, 0:CK], wk_rows[:], ctxT[:, GT * g:GT * g + GT, :],
                   start=True, stop=True).then_inc(k_projected, 1)

            def make_values(b, g):
                if g == 0:
                    pe.wait_ge(q_copied, b + 1)
                elif g == 1:
                    if not (isinstance(b, int) and b < 2):
                        pe.wait_ge(x1_ready, b - 1)
                    pe.wait_ge(val_copied, NG * b + g)
                else:
                    pe.wait_ge(val_copied, NG * b + g)
                for t in range(GT):
                    last = mm(misc_ps[0:KP, t * D:(t + 1) * D], ctxT[:, GT * g + t, :], wv_rows[:],
                              start=True, stop=True)
                last.then_inc(val_done, 1)

            def max_chunk(b, n):
                if n == HALF // P * NG:
                    pe.wait_ge(q_h_ready, 2 * b + 2)
                if n == 0:
                    pe.wait_ge(q_h_ready, 2 * b + 1)
                    pe.wait_ge(k_l_ready, NG * b + 2)
                elif n == 1:
                    pe.wait_ge(k_l_ready, NG * b + 3)
                else:
                    pe.wait_ge(max_reduced, MN * b + n - 1)
                g = n % NG
                mm(prep_ps[:, n % 2, 0:CK], q_h[:].rearrange("p h q -> p (h q)")[:, n // NG * P:(n // NG + 1) * P],
                   key_h[:, GT * g:GT * g + GT, :], start=True, stop=True).then_inc(max_scored, 1)

            def ready_for_max(b, first):
                pe.wait_ge(neg_max_ready, b + 2)
                if first:
                    pe.wait_ge(val_copied, 2 * NG)
                else:
                    pe.wait_ge(x2_l_ready, b)

            def max_row(b):
                nc.tensor.transpose(misc_ps[0:MT, P:2 * P], neg_max[:], ident[:]).then_inc(max_transposed, 1)

            def score_half(b, k, t, n, first):
                if t == 0 and n == 0:
                    pe.wait_ge(k_copied, 16 * 3 * QUADS * b + 16 * 3 * QUADS)
                    pe.wait_ge(q_quad_ready, b + 1)
                    pe.wait_ge(max_placed, 16 * b + 16)
                if n == 0 and not (first and t < 2):
                    pe.wait_ge(exp_done, KT * b + t - 1)
                for g in (2 * n, 2 * n + 1):
                    last = mm(scores_ps[0:KP, t % 2, n, (g % 2) * QN:(g % 2 + 1) * QN], keys[0:SR, k, g, t, :],
                              q_quad[k][0:SR, g], start=True, stop=True)
                if n == 1:
                    last.then_inc(scored, 1)

            def value_half(b, k, t, r, first):
                if r == 0:
                    pe.wait_ge(exp_done, KT * b + t + 1)
                    if t == 0:
                        pe.wait_ge(val_copied, NG * b + NG)
                        if not first:
                            pe.wait_ge(acc_copied, b)
                for j in range(J):
                    p = J * r + j
                    last = mm(pv_ps[VW * j:VW * j + VW, r * PQ:(r + 1) * PQ], val[k][:, t, p, :],
                              prob[t % 2][:, p * PQ:(p + 1) * PQ], start=(t == 0 and r == 0), stop=(t == KT - 1),
                              skip_group_check=True)
                if r == R - 1:
                    last.then_inc(pv_done, 1)

            def value_tile(b, k, t, first):
                for r in range(R):
                    value_half(b, k, t, r, first)

            def transpose_acc(b):
                for r in range(R):
                    for a in range(2):
                        n = 2 * r + a
                        last = nc.tensor.transpose(misc_ps[0:NQ, n * P:(n + 1) * P], acc[:, r, a, :], ident[:])
                last.then_inc(acc_transposed, 1)

            def transpose_heads(b):
                nc.tensor.transpose(misc_ps[:, 0:NQ], heads[:], ident[0:NQ, 0:NQ]).then_inc(heads_transposed, 1)

            def project(b):
                pe.wait_ge(headsT_copied, b + 1)
                mm(misc_ps[0:NQ, 0:D], headsT[:], wo[:], start=True, stop=True).then_inc(projected, 1)

            def make_logits(part):
                for t in range(GATED):
                    o = misc_ps[:, t * NE:(t + 1) * NE]
                    cols = slice((GATED * part + t) * P, (GATED * part + t + 1) * P)
                    mm(o, x2_h[:, cols], wg_h[:], start=True, stop=False)
                    mm(o, x2_h[:, cols], wg_l[:], start=False, stop=False)
                    last = mm(o, x2_l[:, cols], wg_h[:], start=False, stop=True)
                last.then_inc(logits_done, 1)

            def transpose_gates(part, n, bank):
                for t in range(4 * n, min(4 * n + 4, GATED)):
                    last = nc.tensor.transpose(bank[0:2 * NE, (t % 4) * P:(t % 4 + 1) * P],
                                               gate_hl[:, GATED * part + t, :].bitcast(F32), ident[:])
                last.then_inc(gates_transposed, 1)

            def transpose_x2(b):
                nc.tensor.transpose(misc_ps[:, 0:NQ], xn2[:], ident[0:NQ, 0:NQ]).then_inc(x2_transposed, 1)

            pe.wait_ge(consts_ready, 1)
            pe.wait_ge(ones_ready, 2)
            ctx_transpose(0, 0, 0)
            ctx_transpose(0, 0, 1)
            pe.wait_ge(ln_done[0], 1)
            transpose_xn(0)
            pe.wait_ge(wq_ready, 1)
            project_q(0)
            ctx_transpose(0, 0, 2)
            for g in range(NG):
                project_keys(0, g)
            make_values(0, 0)
            for n in range(MN):
                if n == 0:
                    pe.wait_ge(q_h_ready, 2)
                    pe.wait_ge(k_h_ready, NG)
                if n >= 4:
                    pe.wait_ge(max_reduced, n - 3)
                g = n % NG
                mm(scores_ps[:, (n % 4) // 2, n % 2, 0:CK],
                   q_h[:].rearrange("p h q -> p (h q)")[:, n // NG * P:(n // NG + 1) * P],
                   key_h[:, GT * g:GT * g + GT, :], start=True, stop=True).then_inc(max_scored, 1)
                if n in (4, 6):
                    make_values(0, n // 2 - 1)
                if n == 8:
                    pe.wait_ge(k_l_ready, NG)
                    for g in range(NG):
                        ctx_transpose(1, 1, g)
                if n == 10:
                    pe.wait_ge(late_loaded, LATE_LOADS * 16)
                    pe.wait_ge(val_copied, NG)
                    nc.tensor.transpose(misc_ps[:, 0:NU + NE], b_rows[:], ident[0:NU + NE, 0:NU + NE]
                                        ).then_inc(b_transposed, 1)
            project_keys(1, 0)
            pe.wait_ge(xnT_copied, 2)
            pe.wait_ge(ln_done[0], 2)
            project_keys(1, 1)
            transpose_xn(1)
            pe.wait_ge(xnT_copied, 3)
            pe.wait_ge(neg_max_ready, 1)
            max_row(0)
            pe.wait_ge(maxT_ready, 1)
            project_q(1)
            project_keys(1, 2)
            pe.wait_ge(ones_ready, 6)

            def main(b, k, ahead):
                c, d, m, first = b + 1, b + 2, 1 - k, is_first(b)
                for t in range(KT):
                    maxima = MAX_STEPS[t] if ahead >= 1 else 0
                    chunk = sum(MAX_STEPS[:t])
                    if t == 0 and not first:
                        value_tile(b - 1, m, KT - 1, False)
                    score_half(b, k, t, 0, first)
                    score_half(b, k, t, 1, first)
                    if maxima and t == 4 and not first:
                        pe.wait_ge(heads_ready, b)
                    if maxima:
                        max_chunk(c, chunk)
                    if maxima and t == 4 and not first:
                        transpose_heads(b - 1)
                    if ahead >= 2 and t == 10:
                        project_keys(d, 0)
                    if ahead >= 2 and t == 11:
                        project_keys(d, 2)
                    if not first:
                        if t == 2:
                            pe.wait_ge(acc_copied, b)
                            if ahead >= 1:
                                pe.wait_ge(val_copied, NG * c + 1)
                            else:
                                pe.wait_ge(x2_l_ready, b - 1)
                                pe.wait_ge(gate_step, 1)
                        if t == 3 and not maxima:
                            pe.wait_ge(heads_ready, b)
                        if t == 7:
                            pe.wait_ge(ln_done[1], b)
                            if ahead >= 1:
                                pe.wait_ge(val_copied, NG * c + NG)
                    if ahead == 1 and t == 8:
                        ready_for_max(b, first)
                    if t >= 1:
                        value_half(b, k, t - 1, 0, first)
                        if maxima == 3 or (maxima and t == 7):
                            max_chunk(c, chunk + 1)
                        value_half(b, k, t - 1, 1, first)
                    if not first:
                        if t == 2:
                            transpose_acc(b - 1)
                        if t == 3 and not maxima:
                            transpose_heads(b - 1)
                        if t == 4:
                            project(b - 1)
                        if t == 7:
                            transpose_x2(b - 1)
                    if ahead >= 1 and t in VALUE_STEPS:
                        make_values(c, VALUE_STEPS.index(t))
                    if maxima and t != 7:
                        max_chunk(c, chunk + maxima - 1)
                    if ahead >= 2:
                        if t == 8:
                            ctx_transpose(d, k, 0)
                            ready_for_max(b, first)
                            ctx_transpose(d, k, 1)
                        if t == 9:
                            pe.wait_ge(ln_done[0], d + 1)
                            pe.wait_ge(maxT_ready, c + 1)
                            ctx_transpose(d, k, 2)
                            transpose_xn(d)
                        if t == 10:
                            project_q(d)
                            project_keys(d, 1)
                    if ahead >= 1 and t == 8:
                        max_row(c)
                    if ahead == 1 and t == 9:
                        pe.wait_ge(maxT_ready, c + 1)
                        pe.wait_ge(weights_split, 3)
                        make_logits(0)
                    if ahead == 0 and t == 3:
                        pe.wait_ge(gate_step, GATE_STEPS)
                        for n in range(2):
                            transpose_gates(0, n, prep_ps[:, n])

            batches(pe, main)
            value_tile(B - 1, 1, KT - 1, False)

            def hidden(n, u):
                e, s = u // SL, u % SL
                tokens = bass.ds(n * HALF, HALF)
                o = scores_ps[:, (u % 4) // 2, u % 2, 0:HALF]
                wh = w1_h[:, e, s * P:(s + 1) * P]
                mm(o, wh, x2_h[:, tokens], start=True, stop=False)
                mm(o, wh, x2_l[:, tokens], start=False, stop=False)
                mm(o, w1_l[:, e, s * P:(s + 1) * P], x2_h[:, tokens], start=False, stop=True
                   ).then_inc(hidden_done, 1)

            def second(n, u):
                e = (u // SL) % NE
                pe.wait_ge(gelu_l_ready, NU * n + u + 1)
                if isinstance(n, int) and n == 0 and u % SL == 0:
                    pe.wait_ge(w_split, NE + e + 1)
                    if e == 0:
                        pe.wait_ge(acc_copied, B)
                    if e == 3:
                        pe.wait_ge(gate_step, GATE_STEPS + 1)
                if u % SL == 0:
                    if not isinstance(n, int) or e >= 3:
                        pe.wait_ge(scaled, NE * n + e - 1)
                    elif e >= 1:
                        pe.wait_ge(scaled, e)
                o = result_ps(n, e)
                s = u % SLOTS
                high, low = (w2_hl[:, e, a, u % SL, :] for a in range(2))
                mm(o, high, gelu_h[:, s, :], start=(u % SL == 0), stop=False)
                mm(o, high, gelu_l[:, s, :], start=False, stop=False)
                mm(o, low, gelu_h[:, s, :], start=False, stop=(u % SL == SL - 1)
                   ).then_inc(multiplied, 1)

            def chunk(n):
                begin = isinstance(n, int)
                for u in range(NU):
                    if not (begin and u < 4):
                        pe.wait_ge(gelu_done, NU * n + u - 3)
                    if u % SL == 0 and not (begin and u < 2 * SL):
                        pe.wait_ge(spread_copied, NE * n + u // SL - 1)
                    if u == 0 and not begin:
                        pe.wait_ge(gates_copied, 4)
                    if begin:
                        if u == 0:
                            pe.wait_ge(gates_copied, 2)
                            pe.wait_ge(w_split, NE)
                            pe.wait_ge(acc_copied, B)
                            pe.wait_ge(x2_l_ready, B - 1)
                        if u == 3:
                            pe.wait_ge(heads_ready, B)
                        if u == 6:
                            pe.wait_ge(ln_done[1], B)
                        if u == 8:
                            pe.wait_ge(x2_l_ready, B)
                        if u == NU - 2:
                            pe.wait_ge(gate_step, 2 * GATE_STEPS)
                            pe.wait_ge(spread_copied, NE - 1)
                        if u == NU - 1:
                            pe.wait_ge(gates_copied, 3)
                    hidden(n, u)
                    if u % SL == 0:
                        mm(prep_ps[:, (u // SL) % 2, 0:HALF], expert_pick[:, u // SL, :],
                           gT2[:, bass.ds(n * HALF, HALF)], start=True, stop=True).then_inc(spread_done, 1)
                    if begin:
                        if u == 0:
                            transpose_acc(B - 1)
                        if u == 3:
                            transpose_heads(B - 1)
                        if u == 4:
                            project(B - 1)
                        if u == 6:
                            transpose_x2(B - 1)
                        if u == 8:
                            make_logits(1)
                        if u in (NU - 2, NU - 1):
                            transpose_gates(1, u - (NU - 2), prep_ps[:, 0])
                    if not (begin and u < LAG):
                        second(n, u - LAG)

            chunk(0)
            with pe.Fori(1, CH) as n:
                chunk(n)

            for n in range(4):
                if n < 2:
                    pe.wait_ge(gelu_done, CH * NU)
                    pe.wait_ge(summed, NE * (CH - 1))
                if n == 2:
                    for u in range(-LAG, 0):
                        second(CH, u)
                    pe.wait_ge(summed, NE * CH)
                w = min(4, TT - 4 * n)
                for t in range(4 * n, 4 * n + w):
                    last = nc.tensor.transpose(scores_ps[:, n // 2, n % 2, (t % 4) * P:(t % 4 + 1) * P],
                                               sumT[:, t * P:(t + 1) * P], ident[:])
                last.then_inc(y_transposed, 1)


_INS = ['x', 'ctx_768', 'g_xattn', 'g_ffn', 'L0_xattn_Wq', 'L0_xattn_bq', 'L0_xattn_Wk', 'L0_xattn_bk',
        'L0_xattn_Wv', 'L0_xattn_bv', 'L0_xattn_Wo', 'L0_xattn_bo', 'L0_ffn_Wg', 'L0_ffn_bg', 'L0_ffn_W1',
        'L0_ffn_b1', 'L0_ffn_W2', 'L0_ffn_b2']
_OUT = ((32, 56, 128), 'float32')


def kernel(**inputs):
    import numpy as _np
    import concourse.bacc as _bacc
    from concourse import mybir as _mybir
    from concourse.bass_utils import run_bass_kernel_spmd as _run

    nc = _bacc.Bacc("TRN2", target_bir_lowering=False, num_devices=1)
    arrays, args = {}, []
    for name in _INS:
        a = _np.ascontiguousarray(inputs[name])
        arrays[f"in_{name}_dram"] = a
        args.append(nc.dram_tensor(f"in_{name}_dram", a.shape, _mybir.dt.from_np(a.dtype), kind="ExternalInput").ap())
    shape, dtype = _OUT
    out = nc.dram_tensor("out_0_dram", shape, _mybir.dt.from_np(_np.dtype(dtype)), kind="ExternalOutput").ap()
    gated_xattn_moe(nc, *args, out)
    r = _run(nc, [arrays], core_ids=[0])
    return r.results[0]["out_0_dram"]
```
